# Optimizing a Trainium2 kernel written in Bass

```python
import numpy as np
import jax
import jax.numpy as jnp

def _softmax(x, axis=-1):
    return jax.nn.softmax(x, axis=axis)

def _gelu(x):
    return jax.nn.gelu(x, approximate=True)

def _silu(x):
    return jax.nn.silu(x)

def _sigmoid(x):
    return jax.nn.sigmoid(x)

def _layernorm(x, axis=-1, eps=1e-05):
    m = jnp.mean(x, axis=axis, keepdims=True)
    v = jnp.var(x, axis=axis, keepdims=True)
    return (x - m) / jnp.sqrt(v + eps)

def _scatter_add(tgt, idx, src, axis=0):
    return tgt.at[idx].add(src)

def _segment_sum(src, seg, n):
    return jax.ops.segment_sum(src, seg, n)
kernel_name = 'mk_seq_preln_d1_jaxref_r8_cff8ae'

def setup_inputs(seed: int=0):
    np.random.seed(seed)
    _w = jnp.asarray

    def _L0_attn_setup():
        import jax, jax.numpy as jnp
        import numpy as np
        D = 256
        H = 8
        CHUNK = 128
        NORM_GK = 16.0
        EPS = 1e-05

        def _chunked_gla(q, k, v, gk):
            gkc = jnp.cumsum(gk, axis=-2)
            qd = q * jnp.exp(gkc)
            kd = k * jnp.exp(gkc[..., -1:, :] - gkc)
            A = jnp.einsum('bhnid,bhnjd->bhnij', qd, k * jnp.exp(-gkc))
            c = q.shape[-2]
            mask = jnp.tril(jnp.ones((c, c), dtype=bool))
            o_intra = jnp.einsum('bhnij,bhnjv->bhniv', jnp.where(mask, A, 0.0), v)
            decay_last = jnp.exp(gkc[..., -1, :])

            def step(S, inp):
                qd_c, kd_c, v_c, dl = inp
                o1 = jnp.einsum('bhcd,bhdv->bhcv', qd_c, S)
                S = dl[..., :, None] * S + jnp.einsum('bhcd,bhcv->bhdv', kd_c, v_c)
                return (S, o1)
            b, h, n, _, dk = q.shape
            dv = v.shape[-1]
            S0 = jnp.zeros((b, h, dk, dv), q.dtype)
            xs = (jnp.moveaxis(qd, 2, 0), jnp.moveaxis(kd, 2, 0), jnp.moveaxis(v, 2, 0), jnp.moveaxis(decay_last, 2, 0))
            _, o_inter = jax.lax.scan(step, S0, xs)
            o_inter = jnp.moveaxis(o_inter, 0, 2)
            return o_inter + o_intra
        key = jax.random.key(seed)
        ks = jax.random.split(key, 10)
        s = 0.02
        return {'x': jax.random.normal(ks[0], (4, 256, D), jnp.float32), 'Wq': jax.random.normal(ks[1], (D, D // 2), jnp.float32) * s, 'Wk': jax.random.normal(ks[2], (D, D // 2), jnp.float32) * s, 'Wkg1': jax.random.normal(ks[3], (D, 16), jnp.float32) * s, 'Wkg2': jax.random.normal(ks[4], (16, D // 2), jnp.float32) * s, 'bkg2': jnp.zeros((D // 2,), jnp.float32), 'Wv': jax.random.normal(ks[5], (D, D), jnp.float32) * s, 'Wg': jax.random.normal(ks[6], (D, D), jnp.float32) * s, 'bg': jnp.zeros((D,), jnp.float32), 'Wo': jax.random.normal(ks[7], (D, D), jnp.float32) * s}
    _L0_attn_in = _L0_attn_setup()

    def _L0_ffn_setup():
        import jax, jax.numpy as jnp
        import numpy as np
        TOP_P = 0.9
        S, B, H, I, E = (256, 4, 256, 512, 8)

        def _top_p_weights(probs, top_p):
            order = jnp.argsort(-probs, axis=-1)
            sp = jnp.take_along_axis(probs, order, axis=-1)
            cum = jnp.cumsum(sp, axis=-1)
            exceed = cum > top_p
            first_idx = jnp.argmax(exceed, axis=-1)
            first = jnp.arange(probs.shape[-1])[None, :] == first_idx[:, None]
            keep = ~exceed | first
            kept = jnp.where(keep, sp, 0.0)
            t_idx = jnp.arange(probs.shape[0])[:, None]
            return jnp.zeros_like(probs).at[t_idx, order].set(kept)
        key = jax.random.key(seed)
        ks = jax.random.split(key, 5)
        scale = 0.02
        return {'hidden_states': jax.random.normal(ks[0], (S, B, H), dtype=jnp.float32), 'router_w': jax.random.normal(ks[1], (E, H), dtype=jnp.float32) * scale, 'gate_w': jax.random.normal(ks[2], (E, I, H), dtype=jnp.float32) * scale, 'up_w': jax.random.normal(ks[3], (E, I, H), dtype=jnp.float32) * scale, 'down_w': jax.random.normal(ks[4], (E, H, I), dtype=jnp.float32) * scale}
    _L0_ffn_in = _L0_ffn_setup()
    _d = {'L0_attn_x': _L0_attn_in['x'], 'L0_attn_Wq': _L0_attn_in['Wq'], 'L0_attn_Wk': _L0_attn_in['Wk'], 'L0_attn_Wkg1': _L0_attn_in['Wkg1'], 'L0_attn_Wkg2': _L0_attn_in['Wkg2'], 'L0_attn_bkg2': _L0_attn_in['bkg2'], 'L0_attn_Wv': _L0_attn_in['Wv'], 'L0_attn_Wg': _L0_attn_in['Wg'], 'L0_attn_bg': _L0_attn_in['bg'], 'L0_attn_Wo': _L0_attn_in['Wo'], 'L0_ffn_router_w': _L0_ffn_in['router_w'], 'L0_ffn_gate_w': _L0_ffn_in['gate_w'], 'L0_ffn_up_w': _L0_ffn_in['up_w'], 'L0_ffn_down_w': _L0_ffn_in['down_w']}
    _x0 = _d['L0_attn_x']
    _d['L0_attn_x'] = jax.random.normal(jax.random.fold_in(jax.random.key(seed), 1), (2, 1024, 256), dtype=_x0.dtype)
    del _x0
    return _d

def reference(L0_attn_x, L0_attn_Wq, L0_attn_Wk, L0_attn_Wkg1, L0_attn_Wkg2, L0_attn_bkg2, L0_attn_Wv, L0_attn_Wg, L0_attn_bg, L0_attn_Wo, L0_ffn_router_w, L0_ffn_gate_w, L0_ffn_up_w, L0_ffn_down_w):

    def _L0_attn_ref(x, Wq, Wk, Wkg1, Wkg2, bkg2, Wv, Wg, bg, Wo):
        import jax, jax.numpy as jnp
        import numpy as np
        D = 256
        H = 8
        CHUNK = 128
        NORM_GK = 16.0
        EPS = 1e-05

        def _chunked_gla(q, k, v, gk):
            gkc = jnp.cumsum(gk, axis=-2)
            qd = q * jnp.exp(gkc)
            kd = k * jnp.exp(gkc[..., -1:, :] - gkc)
            A = jnp.einsum('bhnid,bhnjd->bhnij', qd, k * jnp.exp(-gkc))
            c = q.shape[-2]
            mask = jnp.tril(jnp.ones((c, c), dtype=bool))
            o_intra = jnp.einsum('bhnij,bhnjv->bhniv', jnp.where(mask, A, 0.0), v)
            decay_last = jnp.exp(gkc[..., -1, :])

            def step(S, inp):
                qd_c, kd_c, v_c, dl = inp
                o1 = jnp.einsum('bhcd,bhdv->bhcv', qd_c, S)
                S = dl[..., :, None] * S + jnp.einsum('bhcd,bhcv->bhdv', kd_c, v_c)
                return (S, o1)
            b, h, n, _, dk = q.shape
            dv = v.shape[-1]
            S0 = jnp.zeros((b, h, dk, dv), q.dtype)
            xs = (jnp.moveaxis(qd, 2, 0), jnp.moveaxis(kd, 2, 0), jnp.moveaxis(v, 2, 0), jnp.moveaxis(decay_last, 2, 0))
            _, o_inter = jax.lax.scan(step, S0, xs)
            o_inter = jnp.moveaxis(o_inter, 0, 2)
            return o_inter + o_intra
        b, T, _ = x.shape
        n = T // CHUNK
        dk = D // 2 // H
        dv = D // H
        scaling = (D // H) ** (-0.5)
        q = x @ Wq
        k = x @ Wk * scaling
        gk = jax.nn.log_sigmoid(x @ Wkg1 @ Wkg2 + bkg2) / NORM_GK
        v = x @ Wv
        g = x @ Wg + bg

        def split(t, hd):
            return t.reshape(b, n, CHUNK, H, hd).transpose(0, 3, 1, 2, 4)
        o = _chunked_gla(split(q, dk), split(k, dk), split(v, dv), split(gk, dk))
        mu = o.mean(-1, keepdims=True)
        var = o.var(-1, keepdims=True)
        o = (o - mu) / jnp.sqrt(var + EPS)
        o = o.transpose(0, 2, 3, 1, 4).reshape(b, T, D)
        o = jax.nn.silu(g) * o
        return o @ Wo

    def _L0_ffn_ref(hidden_states, router_w, gate_w, up_w, down_w):
        import jax, jax.numpy as jnp
        import numpy as np
        TOP_P = 0.9
        S, B, H, I, E = (256, 4, 256, 512, 8)

        def _top_p_weights(probs, top_p):
            order = jnp.argsort(-probs, axis=-1)
            sp = jnp.take_along_axis(probs, order, axis=-1)
            cum = jnp.cumsum(sp, axis=-1)
            exceed = cum > top_p
            first_idx = jnp.argmax(exceed, axis=-1)
            first = jnp.arange(probs.shape[-1])[None, :] == first_idx[:, None]
            keep = ~exceed | first
            kept = jnp.where(keep, sp, 0.0)
            t_idx = jnp.arange(probs.shape[0])[:, None]
            return jnp.zeros_like(probs).at[t_idx, order].set(kept)
        s, b, h = hidden_states.shape
        x = hidden_states.reshape(-1, h)
        probs = jax.nn.softmax(x @ router_w.T, axis=-1)
        w = _top_p_weights(probs, TOP_P)
        out = jnp.zeros_like(x)
        n_exp = router_w.shape[0]
        for e in range(n_exp):
            g = jax.nn.silu(x @ gate_w[e].T)
            u = x @ up_w[e].T
            y = g * u @ down_w[e].T
            out = out + y * w[:, e:e + 1]
        return out.reshape(s, b, h)
    x = L0_attn_x
    x = x + _L0_attn_ref(_layernorm(x, axis=-1), L0_attn_Wq, L0_attn_Wk, L0_attn_Wkg1, L0_attn_Wkg2, L0_attn_bkg2, L0_attn_Wv, L0_attn_Wg, L0_attn_bg, L0_attn_Wo)
    x = x + _L0_ffn_ref(_layernorm(x, axis=-1), L0_ffn_router_w, L0_ffn_gate_w, L0_ffn_up_w, L0_ffn_down_w)
    return x

_drawn_inputs = setup_inputs


def setup_inputs(seed=0):
    import zlib

    import numpy as np

    out = dict(_drawn_inputs(seed))
    spreads = {'L0_attn_bkg2': (0.0, 0.8), 'L0_attn_bg': (0.0, 0.486)}
    factors = {'L0_attn_Wkg1': 8.0,
     'L0_attn_Wkg2': 8.0,
     'L0_ffn_router_w': 8.0,
     'L0_ffn_gate_w': 6.517,
     'L0_ffn_up_w': 6.425,
     'L0_ffn_down_w': 6.435}
    for name, (base, spread) in spreads.items():
        noise = np.random.default_rng([zlib.crc32(name.encode()), seed]).standard_normal(out[name].shape)
        drawn = base * np.exp(spread * noise) if base else spread * noise
        out[name] = jnp.asarray(drawn.astype(out[name].dtype))
    for name, factor in factors.items():
        out[name] = (out[name] * factor).astype(out[name].dtype)
    return out
```

```python
import concourse.bass as bass
from concourse import mybir
from contextlib import ExitStack


def gla_moe_layer(nc, x, Wq, Wk, Wkg1, Wkg2, bkg2, Wv, Wg, bg, Wo, rw, gate_w, up_w, down_w, out):
    F32 = mybir.dt.float32
    ALU = mybir.AluOpType
    ACT = mybir.ActivationFunctionType
    AX = mybir.AxisListType
    P = 128
    NB, T, D = 2, 1024, 256
    NCH = T // P
    H = 8
    DK, DV = 128 // H, D // H
    HALF = D // 2
    KD = D // P
    R = 16
    E = 8
    SCALING = float(DV) ** -0.5
    GK = 1.0 / 16.0
    EPS = 1e-5
    TOP_P = 0.9
    F32R = mybir.dt.float32r
    F16 = mybir.dt.float16
    I32 = mybir.dt.int32
    U32 = mybir.dt.uint32
    NT = NB * NCH
    TOK = NB * T
    I = 512
    IC = I // P
    WN = KD * I
    ROW = D + E
    MINT = 2

    rows = nc.dram_tensor("token_rows", (TOK + P, ROW), F32, kind="Internal").ap()
    acc = nc.dram_tensor("token_sums", (TOK + P, D), F32, kind="Internal").ap()

    with ExitStack() as ctx:
        def sb(name, shape, dt=F32):
            return ctx.enter_context(nc.sbuf_tensor(name, shape, dt))

        def sem(name):
            return ctx.enter_context(nc.semaphore(name))

        xs = sb("xs", [P, NB, NCH * D])
        wq = sb("wq", [P, KD, HALF]); wk = sb("wk", [P, KD, HALF])
        wv = sb("wv", [P, KD, D]); wg = sb("wg", [P, KD, D]); wo = sb("wo", [P, KD, D])
        wkg1 = sb("wkg1", [P, KD, R]); wkg2 = sb("wkg2", [R, HALF])
        bkg2_row = sb("bkg2_row", [1, HALF]); bg_row = sb("bg_row", [1, D])
        rw_sb = sb("rw_sb", [P, KD, E])
        ident = sb("ident", [P, P]); upto = sb("upto", [P, P]); after = sb("after", [P, P])
        head_rows = sb("head_rows", [P, H]); head_block = sb("head_block", [P, D])
        ones_row = sb("ones_row", [1, P])
        stats = sb("stats", [P, NB, 6 * NCH]); mv = sb("mv", [P, NB, NCH, 2]); vare = sb("vare", [P, NB, NCH]); rstd = sb("rstd", [P, NB, NCH])
        x2 = sb("x2", [P, NB, D]); sum2 = sb("sum2", [P, NB, 1]); negmean2 = sb("negmean2", [P, NB, 1]); ssq2 = sb("ssq2", [P, NB, 1]); sq2 = sb("sq2", [P, NB, D]); vare2 = sb("vare2", [P, NB, 1]); rstd2 = sb("rstd2", [P, NB, 1])
        minus_half = sb("minus_half", [P, 2 * NCH])
        xn = sb("xn", [P, NB, D]); xnT = sb("xnT", [P, NB, KD * P])
        g1T = sb("g1T", [R, NB, P]); qkT = sb("qkT", [P, NB, 2 * P])
        vk = sb("vk", [P, NB, D + HALF])
        za = sb("za", [P, NB, HALF]); zr = sb("zr", [P, NB, HALF]); ze = sb("ze", [P, NB, HALF])
        zl = sb("zl", [P, NB, HALF]); gneg = sb("gneg", [P, NB, HALF])
        work = sb("work", [P, NB * (2 * H * P + 8 * D)])
        taken = [0]

        def part(width):
            at = taken[0]
            taken[0] += NB * width
            return work[:, at:at + NB * width].rearrange("p (b n) -> p b n", b=NB)
        gs = part(D); ge = part(D); gt = part(D); sg = part(D); gd = part(D)
        e1 = sb("e1", [P, NB, P]); e2 = sb("e2", [P, NB, P]); e3 = sb("e3", [P, NB, HALF])
        qd = sb("qd", [P, NB, P]); kn = sb("kn", [P, NB, P]); kd = sb("kd", [P, NB, HALF])
        qm = part(H * P); am = part(H * P)
        st = sb("st", [P, NB, D]); su = sb("su", [P, NB, D])
        hsum = sb("hsum", [P, NB, H]); hmean = sb("hmean", [P, NB, H])
        oc = part(D); osq = part(D); on = part(D)
        hvar = sb("hvar", [P, NB, H]); hrs = sb("hrs", [P, NB, H])
        og = sb("og", [P, NB, D]); ogT = sb("ogT", [P, NB, KD * P])
        x2n = sb("x2n", [P, NB, D]); x2nT = sb("x2nT", [P, NB, KD * P])
        logits = sb("logits", [P, NB, NCH * E])

        pe8 = lambda name, dt=F32: sb(name, [P, NT, E], dt)
        probs = pe8("probs"); expo = pe8("expo"); lmax = sb("lmax", [P, NT]); lsum = sb("lsum", [P, NT]); lrec = sb("lrec", [P, NT])
        shifted = pe8("shifted"); wts = pe8("wts"); before = sb("before", [P, NT, E]); 
        pg = sb("pg", [P, NT, E, E]); pq = sb("pq", [P, NT, E, E]); earlier = sb("earlier", [P, E, E])
        keep = sb("keep", [P, E, NT]); tot = sb("tot", [P, E, NT]); scan = [sb(f"scan{i}", [P, E, NT]) for i in range(2)]
        slot = sb("slot", [P, E, NT]); slot_i = sb("slot_i", [P, E, NT], I32); sb_i = sb("sb_i", [P, E, NT], I32); sa_i = sb("sa_i", [P, E, NT], I32)
        slot_b = sb("slot_b", [P, E * NT]); slot_a = sb("slot_a", [P, E, NT])
        tril = sb("tril", [P, P]); ones = sb("ones", [P, P])
        iota_b = sb("iota_b", [P, P], F16); iota_a = sb("iota_a", [P, NT]); tok_id = sb("tok_id", [P, NT]); dummy = sb("dummy_row", [P, 1])
        hot_a = sb("hot_a", [P, E * NT, NT]); id_a = sb("id_a", [P, E * NT * NT], F16); hot_b = work[:, 0:E * NT * P // 2].bitcast(F16)
        empty = sb("empty", [P, E * NT]); lists = sb("lists", [P, E * NT], U32)
        tiles_i = sb("tiles_i", [P, E], I32); tiles_s = sb("tiles_s", [P, E], I32); tiles_f = [sb(f"tiles_f{i}", [P, E]) for i in range(2)]
        starts = sb("starts", [P, E + 1], I32)
        zrow = sb("zrow", [P, ROW])
        raw = sb("raw", [P, 3 * WN])
        whi = [sb(f"whi{q}", [P, 3 * WN], F32R) for q in range(2)]; wlo = [sb(f"wlo{q}", [P, 3 * WN], F32R) for q in range(2)]
        flat = sb("flat", [P, E * NT + 4], U32); idx_g = sb("idx_g", [P, 1], U32); idx_s = sb("idx_s", [P, 1], U32)
        xg = sb("xg", [P, ROW]); wcur = sb("wcur", [P, E])
        xhi = sb("xhi", [P, KD * P], F32R); xlo = sb("xlo", [P, KD * P], F32R)
        gact = sb("gact", [P, I]); hid = sb("hid", [P, I]); hhi = sb("hhi", [P, I], F32R); hlo = sb("hlo", [P, I], F32R)
        ybuf = sb("ybuf", [P, D])

        pa = [ctx.enter_context(nc.psum_tensor(f"pa{b}", [P, 512], F32)) for b in range(NB)]
        pc = [ctx.enter_context(nc.psum_tensor(f"pc{b}", [P, 512], F32)) for b in range(NB)]
        pde = [ctx.enter_context(nc.psum_tensor(f"pde{b}", [P, 1024], F32)) for b in range(NB)]

        S = {}
        for name in ("x_in w_q w_k w_kg1 w_kg2 w_v w_g w_o w_r const memz "
                     "stats_d mv_d vare_d vare2_d rstd_d xn_d xnT_ps xnT_d qkg_ps g1T_d qkT_d vk_ps vk_d "
                     "zg_ps za_d zr_d ze_d zl_d gneg_d gs_d ge_d gt_d gd_d sg_d cum_ps e1_d e2_d e3_d "
                     "qd_d kn_d kd_d qm_d a_ps am_d so_ps su_d st_d hsum_d hmean_d oc_d osq_d hvar_d hvs_d hrs_d "
                     "on_d og_d ogT_ps ogT_d y_ps x2_d x2_st0 x2_st1 mean2_d ssq2_d rstd2_d x2n_d x2nT_ps x2nT_d lg_ps lg_d out_st "
                     "lmax_d shift_d expo_d lsum_d lrec_d probs_d rank_d before_d wts_d keep_d w_st rows_z pos_ps tot_d scan_d slot_d "
                     "sloti_d slotba_d slotf_d hota_d ida_d hotb_d list_ps empty_d lists_d starts_d xn_st0 xn_st1 "
                     "raw_in whi_d wlo_d gath flat_d idxg_d idxs_d x_ps xhi_d xlo_d wcur_d g_ps sg_done u_ps hid_d ht_ps hhi_d hlo_d yps yev scat moe_c moe_z pass_").split():
            S[name] = sem(name)
        block = ctx.enter_context(nc.Block())

        pG = pde[0][:, 0:I]; pU = pde[0][:, I:2 * I]; pXT = pa[0]; pHT = pa[1]; pY = pc[0]
        pPos = pde[1][:, 0:P]; pTot = pde[1][:, 512:512 + P]; pList = pc[1]

        @block.sync
        def _(e):
            for b in range(NB):
                for hf in range(2):
                    e.dma_start(xs[:, b, hf * 1024:(hf + 1) * 1024].rearrange("p (n d) -> p n d", d=D),
                                x[b, hf * 512:(hf + 1) * 512].rearrange("(n p) d -> p n d", p=P)).then_inc(S["x_in"], 16)
            def load_expert(ei):
                for m, w in enumerate((gate_w, up_w, down_w)):
                    e.dma_start(raw[:, m * WN:(m + 1) * WN].rearrange("p (c n) -> p c n", c=w.shape[1] // P),
                                w[bass.ds(ei, 1)].rearrange("a (c p) n -> p (a c) n", p=P)).then_inc(S["raw_in"], 16)
            load_expert(0)
            e.wait_ge(S["moe_z"], 1)
            e.dma_start(rows[TOK:TOK + P, :], zrow[:]).then_inc(S["rows_z"], 16)
            e.dma_start(acc[TOK:TOK + P, :], zrow[:, 0:D]).then_inc(S["rows_z"], 16)
            for b in range(NB):
                e.sem_inc(S[f"x2_st{b}"], 16)
                e.sem_inc(S[f"xn_st{b}"], 16)
            with e.Fori(0, NCH) as n:
                for b in range(NB):
                    r0 = b * T + n * P
                    e.wait_ge(S["x2_d"], 2 * n + (b + 1))
                    e.dma_start(acc[bass.ds(r0, P), :], x2[:, b, :]).then_inc(S[f"x2_st{b}"], 16)
                for b in range(NB):
                    r0 = b * T + n * P
                    e.wait_ge(S["x2n_d"], 2 * n + (b + 1))
                    e.dma_start(rows[bass.ds(r0, P), 0:D], x2n[:, b, :]).then_inc(S[f"xn_st{b}"], 16)
            e.wait_ge(S["wts_d"], 1)
            e.dma_start(rows[0:TOK, D:ROW].rearrange("(t p) c -> p t c", p=P), wts[:]).then_inc(S["w_st"], 16)
            with e.Fori(1, E) as ei:
                e.wait_ge(S["wlo_d"], 3 * ei)
                load_expert(ei)
            e.wait_ge(S["starts_d"], 2)
            n_tiles = e.value_load(starts[0:1, E:E + 1], min_val=MINT * E, max_val=NT * E)
            e.wait_ge(S["scat"], 16 * n_tiles + 32)
            e.dma_start(out.rearrange("b t d -> (b t) d"), acc[0:TOK, :]).then_inc(S["out_st"], 16)
            e.wait_ge(S["out_st"], 16)

        @block.gpsimd
        def _(e):
            e.memset(ones_row[:], 1.0).then_inc(S["const"], 1)
            e.memset(minus_half[:], -0.5).then_inc(S["const"], 1)
            e.memset(ident[:], 0.0).then_inc(S["memz"], 1)
            e.memset(upto[:], 1.0).then_inc(S["memz"], 1)
            e.memset(after[:], 1.0).then_inc(S["memz"], 1)
            e.memset(head_rows[:], 1.0).then_inc(S["memz"], 1)
            e.memset(head_block[:], 1.0).then_inc(S["memz"], 1)
            e.memset(st[:], 0.0).then_inc(S["const"], 1)
            e.memset(zrow[:], 0.0).then_inc(S["moe_z"], 1)
            e.memset(ybuf[:], 0.0).then_inc(S["moe_c"], 1)
            e.memset(ones[:], 1.0).then_inc(S["moe_c"], 1)
            e.memset(tril[:], 1.0).then_inc(S["memz"], 1)
            e.memset(earlier[:], 1.0).then_inc(S["memz"], 1)
            e.iota(iota_b[:], pattern=[[1, P]], base=0, channel_multiplier=0, allow_small_or_imprecise_dtypes=True).then_inc(S["moe_c"], 1)
            e.iota(iota_a[:], pattern=[[1, NT]], base=0, channel_multiplier=0, allow_small_or_imprecise_dtypes=True).then_inc(S["moe_c"], 1)
            e.iota(tok_id[:], pattern=[[P, NT]], base=1, channel_multiplier=1, allow_small_or_imprecise_dtypes=True).then_inc(S["moe_c"], 1)
            e.iota(dummy[:], pattern=[[1, 1]], base=TOK + 1, channel_multiplier=1, allow_small_or_imprecise_dtypes=True).then_inc(S["moe_c"], 1)
            e.iota(flat[:].bitcast(I32), pattern=[[0, E * NT + 4]], base=TOK, channel_multiplier=1).then_inc(S["moe_c"], 1)
            e.wait_ge(S["memz"], 7)
            e.affine_select(out=ident[:], in_=ident[:], compare_op=ALU.not_equal, fill=1.0, base=0,
                            pattern=[[-1, P]], channel_multiplier=1).then_inc(S["const"], 1)
            e.affine_select(out=upto[:], in_=upto[:], compare_op=ALU.is_ge, fill=0.0, base=0,
                            pattern=[[1, P]], channel_multiplier=-1).then_inc(S["const"], 1)
            e.affine_select(out=tril[:], in_=tril[:], compare_op=ALU.is_gt, fill=0.0, base=0,
                            pattern=[[1, P]], channel_multiplier=-1).then_inc(S["moe_c"], 1)
            e.affine_select(out=earlier[:], in_=earlier[:], compare_op=ALU.is_gt, fill=0.0, base=0,
                            pattern=[[1, E], [-1, E]], channel_multiplier=0).then_inc(S["moe_c"], 1)
            e.affine_select(out=after[:], in_=after[:], compare_op=ALU.is_gt, fill=0.0, base=0,
                            pattern=[[-1, P]], channel_multiplier=1).then_inc(S["const"], 1)
            e.affine_select(out=head_rows[:], in_=head_rows[:], compare_op=ALU.is_ge, fill=0.0, base=0,
                            pattern=[[-DK, H]], channel_multiplier=1).then_inc(S["memz"], 1)
            e.affine_select(out=head_block[:], in_=head_block[:], compare_op=ALU.is_ge, fill=0.0, base=0,
                            pattern=[[-DK, H], [0, DV]], channel_multiplier=1).then_inc(S["memz"], 1)
            e.wait_ge(S["memz"], 9)
            e.affine_select(out=head_rows[:], in_=head_rows[:], compare_op=ALU.is_ge, fill=0.0, base=DK - 1,
                            pattern=[[DK, H]], channel_multiplier=-1).then_inc(S["const"], 1)
            e.affine_select(out=head_block[:], in_=head_block[:], compare_op=ALU.is_ge, fill=0.0, base=DK - 1,
                            pattern=[[DK, H], [0, DV]], channel_multiplier=-1).then_inc(S["const"], 1)
            e.wait_ge(S["const"], 8)
            e.wait_ge(S["vare_d"], 1)
            e.tensor_tensor(rstd[:].rearrange("p b n -> p (b n)"), vare[:].rearrange("p b n -> p (b n)"), minus_half[:], ALU.pow).then_inc(S["rstd_d"], 1)
            with e.Fori(0, NCH) as n:
                for b in range(NB):
                    v = 2 * n + (b + 1)
                    e.wait_ge(S["qd_d"], v)
                    e.tensor_tensor(qm[:, b, :].rearrange("p (h i) -> p h i", h=H),
                                    qd[:, b, :].unsqueeze(1).broadcast_to([P, H, P]),
                                    head_rows[:].unsqueeze(2).broadcast_to([P, H, P]), ALU.mult).then_inc(S["qm_d"], 1)
                for b in range(NB):
                    v = 2 * n + (b + 1)
                    e.wait_ge(S["oc_d"], v)
                    e.tensor_tensor(osq[:, b, :], oc[:, b, :], oc[:, b, :], ALU.mult).then_inc(S["osq_d"], 1)
                for b in range(NB):
                    v = 2 * n + (b + 1)
                    e.wait_ge(S["hvs_d"], v)
                    e.tensor_tensor(hrs[:, b, :], hvar[:, b, :], minus_half[:, 0:H], ALU.pow).then_inc(S["hrs_d"], 1)
                for b in range(NB):
                    v = 2 * n + (b + 1)
                    e.wait_ge(S["vare2_d"], v)
                    e.tensor_tensor(rstd2[:, b, :], vare2[:, b, :], minus_half[:, 0:1], ALU.pow).then_inc(S["rstd2_d"], 1)

            e.wait_ge(S["moe_c"], 9)
            e.sem_inc(S["yev"], 2)
            e.sem_inc(S["x_ps"], 1)
            e.sem_inc(S["wcur_d"], 1)
            e.wait_ge(S["w_st"], 16)
            e.wait_ge(S["rows_z"], 32)
            for b in range(NB):
                e.wait_ge(S[f"x2_st{b}"], 16 * NCH + 16)
                e.wait_ge(S[f"xn_st{b}"], 16 * NCH + 16)
            e.wait_ge(S["lists_d"], 1)
            e.wait_ge(S["starts_d"], 2)

            for ei in range(E):
                t0 = 0 if ei == 0 else e.value_load(starts[0:1, ei:ei + 1], min_val=MINT, max_val=NT * (E - 1))
                e.tensor_copy(flat[:, bass.ds(t0 + 2, NT)], lists[:, ei * NT:(ei + 1) * NT]).then_inc(S["flat_d"], 1)
                e.wait_ge(S["flat_d"], ei + 1)

            def gather(i):
                e.wait_ge(S["x_ps"], i + 1)
                e.sem_inc(S["pass_"], 1)
                e.tensor_copy(idx_g[:], flat[:, bass.ds(i + 2, 1)]).then_inc(S["idxg_d"], 1)
                e.wait_ge(S["wcur_d"], i + 1)
                e.wait_ge(S["idxg_d"], i + 1)
                e.sem_inc(S["pass_"], 1)
                e.indirect_dma_start(out=xg[:], out_offset=None, in_=rows[:, :],
                                     in_offset=bass.IndirectOffsetOnAxis(ap=idx_g[:], axis=0)).then_inc(S["gath"], 16)

            def scatter(i, first=False):
                if not first:
                    e.wait_ge(S["scat"], 16 * i)
                e.sem_inc(S["pass_"], 1)
                e.tensor_copy(idx_s[:], flat[:, bass.ds(i, 1)]).then_inc(S["idxs_d"], 1)
                e.wait_ge(S["idxs_d"], i + 1)
                e.wait_ge(S["yev"], i + 1)
                e.sem_inc(S["pass_"], 1)
                e.indirect_dma_start(out=acc[:, :], out_offset=bass.IndirectOffsetOnAxis(ap=idx_s[:], axis=0),
                                     in_=ybuf[:], in_offset=None, compute_op=ALU.add).then_inc(S["scat"], 16)

            gather(0)
            scatter(0, first=True)
            n_tiles = e.value_load(starts[0:1, E:E + 1], min_val=MINT * E, max_val=NT * E)
            with e.Fori(1, n_tiles + 1) as i:
                gather(i)
                scatter(i)
            scatter(n_tiles + 1)

        @block.scalar
        def _(e):
            for dst, src, s in ((wq, Wq, "w_q"), (wk, Wk, "w_k"), (wkg1, Wkg1, "w_kg1"), (wv, Wv, "w_v"), (wg, Wg, "w_g"), (wo, Wo, "w_o"), (rw_sb, rw, "w_r")):
                e.dma_start(dst[:], src.rearrange("(k p) n -> p k n", p=P)).then_inc(S[s], 16)
            e.dma_start(wkg2[:], Wkg2).then_inc(S["w_kg2"], 16)
            e.dma_start(bkg2_row[:], bkg2.rearrange("(a n) -> a n", a=1)).then_inc(S["w_kg2"], 16)
            e.dma_start(bg_row[:], bg.rearrange("(a n) -> a n", a=1)).then_inc(S["w_kg2"], 16)
            def split_hi(ei, q):
                for m in range(3):
                    e.wait_ge(S["raw_in"], 48 * ei + 48)
                    e.activation(whi[q][:, m * WN:(m + 1) * WN], raw[:, m * WN:(m + 1) * WN], ACT.Copy).then_inc(S["whi_d"], 1)
            split_hi(0, 0)
            e.preload_act_table_set("natural_log_exp_and_others")
            with e.Fori(0, NCH) as n:
                v = [2 * n + (b + 1) for b in range(NB)]
                for b in range(NB):
                    e.wait_ge(S["xnT_ps"], v[b])
                    e.activation(xnT[:, b, :], pa[b][:, 0:256], ACT.Copy).then_inc(S["xnT_d"], 1)
                for b in range(NB):
                    e.wait_ge(S["qkg_ps"], v[b])
                    e.activation(g1T[:, b, :], pa[b][0:R, 0:P], ACT.Copy).then_inc(S["g1T_d"], 1)
                    e.activation(qkT[:, b, :], pa[b][:, 256:512], ACT.Copy).then_inc(S["qkT_d"], 1)
                for b in range(NB):
                    e.wait_ge(S["zg_ps"], v[b])
                    e.activation(za[:, b, :], pde[b][:, 0:HALF], ACT.Abs).then_inc(S["za_d"], 1)
                    e.activation(zr[:, b, :], pde[b][:, 0:HALF], ACT.Relu, scale=-1.0).then_inc(S["zr_d"], 1)
                    e.wait_ge(S["za_d"], v[b])
                    e.activation(ze[:, b, :], za[:, b, :], ACT.Exp, scale=-1.0).then_inc(S["ze_d"], 1)
                    e.activation(ge[:, b, :], pde[b][:, HALF:HALF + D], ACT.Exp, scale=-1.0).then_inc(S["ge_d"], 1)
                    e.wait_ge(S["ze_d"], v[b])
                    e.activation(zl[:, b, :], ze[:, b, :], ACT.Ln, bias=1.0).then_inc(S["zl_d"], 1)
                    e.activation(gs[:, b, :], pde[b][:, HALF:HALF + D], ACT.Copy).then_inc(S["gs_d"], 1)
                for b in range(NB):
                    e.wait_ge(S["cum_ps"], v[b])
                    e.activation(e1[:, b, :], pde[b][:, 512:512 + P], ACT.Exp, scale=-GK).then_inc(S["e1_d"], 1)
                    e.activation(e2[:, b, :], pde[b][:, 512:512 + P], ACT.Exp, scale=GK).then_inc(S["e2_d"], 1)
                    e.activation(e3[:, b, :], pde[b][:, 512 + P:512 + P + HALF], ACT.Exp, scale=-GK).then_inc(S["e3_d"], 1)
                for b in range(NB):
                    e.wait_ge(S["ogT_ps"], v[b])
                    e.activation(ogT[:, b, :], pa[b][:, 0:256], ACT.Copy).then_inc(S["ogT_d"], 1)
                for b in range(NB):
                    e.wait_ge(S["mean2_d"], v[b])
                    e.activation(sq2[:, b, :], x2[:, b, :], ACT.Square, bias=negmean2[:, b, :], accum_out=ssq2[:, b, :]).then_inc(S["ssq2_d"], 1)
                for b in range(NB):
                    e.wait_ge(S["x2nT_ps"], v[b])
                    e.activation(x2nT[:, b, :], pa[b][:, 0:256], ACT.Copy).then_inc(S["x2nT_d"], 1)
            e.wait_ge(S["shift_d"], 1)
            e.activation(expo[:], shifted[:], ACT.Exp).then_inc(S["expo_d"], 1)
            e.preload_act_table_set("silu_and_others")
            e.wait_ge(S["x_ps"], 2)
            e.activation(xhi[:], pXT[:, 0:KD * P], ACT.Copy).then_inc(S["xhi_d"], 1)
            e.wait_ge(S["starts_d"], 2)

            def act_tile(i, first):
                if not first:
                    e.wait_ge(S["hid_d"], i)
                e.wait_ge(S["g_ps"], i + 1)
                e.activation(gact[:], pG[:], ACT.Silu).then_inc(S["sg_done"], 1)
                if not first:
                    e.wait_ge(S["ht_ps"], i)
                    e.activation(hhi[:], pHT[:], ACT.Copy).then_inc(S["hhi_d"], 1)
                e.wait_ge(S["x_ps"], i + 3)
                e.activation(xhi[:], pXT[:, 0:KD * P], ACT.Copy).then_inc(S["xhi_d"], 1)
                if not first:
                    sum_out(i)

            def sum_out(i):
                e.wait_ge(S["scat"], 16 * i + 16)
                e.wait_ge(S["yps"], i)
                e.activation(ybuf[:], pY[:, 0:D], ACT.Copy).then_inc(S["yev"], 1)

            def act_pair(pr, first, more):
                for q in range(2):
                    ei = 2 * pr + q
                    t0 = e.value_load(starts[0:1, bass.ds(ei, 1)], min_val=0, max_val=NT * E) if not (first and q == 0) else 0
                    t1 = e.value_load(starts[0:1, bass.ds(ei + 1, 1)], min_val=MINT, max_val=NT * E)
                    act_tile(t0, first and q == 0)
                    if more or q == 0:
                        split_hi(ei + 1, 1 - q)
                    with e.Fori(t0 + 1, t1) as i:
                        act_tile(i, False)

            act_pair(0, True, True)
            with e.Fori(1, E // 2 - 1) as pr:
                act_pair(pr, False, True)
            act_pair(E // 2 - 1, False, False)
            n_tiles = e.value_load(starts[0:1, E:E + 1], min_val=MINT * E, max_val=NT * E)
            e.wait_ge(S["ht_ps"], n_tiles)
            e.activation(hhi[:], pHT[:], ACT.Copy).then_inc(S["hhi_d"], 1)
            sum_out(n_tiles)

        @block.vector
        def _(e):
            def split_lo(ei, q):
                for m in range(3):
                    e.wait_ge(S["whi_d"], 3 * ei + (m + 1))
                    e.tensor_tensor(wlo[q][:, m * WN:(m + 1) * WN], raw[:, m * WN:(m + 1) * WN],
                                    whi[q][:, m * WN:(m + 1) * WN].bitcast(F32), ALU.subtract).then_inc(S["wlo_d"], 1)
            e.wait_ge(S["x_in"], 64)
            split_lo(0, 0)
            with e.Fori(0, NCH) as n:
                for b in range(NB):
                    e.bn_stats(stats[:, b, bass.ds(n * 6, 6)], xs[:, b, bass.ds(n * D, D)]).then_inc(S["stats_d"], 1)
            e.wait_ge(S["stats_d"], 2 * NCH)
            for b in range(NB):
                for n in range(NCH):
                    e.bn_aggr(mv[:, b, n, :], stats[:, b, n * 6:n * 6 + 6]).then_inc(S["mv_d"], 1)
            e.wait_ge(S["mv_d"], 2 * NCH)
            e.tensor_scalar(vare[:], mv[:, :, :, 1], EPS, None, ALU.add).then_inc(S["vare_d"], 1)
            e.wait_ge(S["rstd_d"], 1)
            e.wait_ge(S["const"], 8)
            with e.Fori(0, NCH) as n:
                v = [2 * n + (b + 1) for b in range(NB)]
                xt = [xs[:, b, bass.ds(n * D, D)] for b in range(NB)]
                for b in range(NB):
                    e.tensor_scalar(xn[:, b, :], xt[b], mv[:, b, bass.ds(n, 1), 0], rstd[:, b, bass.ds(n, 1)],
                                    ALU.subtract, ALU.mult).then_inc(S["xn_d"], 1)
                for b in range(NB):
                    e.wait_ge(S["vk_ps"], v[b])
                    e.tensor_copy(vk[:, b, :], pc[b][:, 0:D + HALF]).then_inc(S["vk_d"], 1)
                for b in range(NB):
                    e.wait_ge(S["zr_d"], v[b])
                    e.wait_ge(S["zl_d"], v[b])
                    e.tensor_tensor(gneg[:, b, :], zr[:, b, :], zl[:, b, :], ALU.add).then_inc(S["gneg_d"], 1)
                for b in range(NB):
                    e.wait_ge(S["ge_d"], v[b])
                    e.tensor_scalar(gt[:, b, :], ge[:, b, :], 1.0, None, ALU.add).then_inc(S["gt_d"], 1)
                    e.wait_ge(S["gt_d"], v[b])
                    e.reciprocal(gd[:, b, :], gt[:, b, :]).then_inc(S["gd_d"], 1)
                    e.wait_ge(S["gd_d"], v[b])
                    e.wait_ge(S["gs_d"], v[b])
                    e.tensor_tensor(sg[:, b, :], gs[:, b, :], gd[:, b, :], ALU.mult).then_inc(S["sg_d"], 1)
                for b in range(NB):
                    e.wait_ge(S["qkT_d"], v[b])
                    e.wait_ge(S["e1_d"], v[b])
                    e.tensor_tensor(qd[:, b, :], qkT[:, b, 0:P], e1[:, b, :], ALU.mult).then_inc(S["qd_d"], 1)
                    e.wait_ge(S["e2_d"], v[b])
                    e.scalar_tensor_tensor(kn[:, b, :], qkT[:, b, P:2 * P], SCALING, e2[:, b, :], ALU.mult, ALU.mult).then_inc(S["kn_d"], 1)
                    e.wait_ge(S["e3_d"], v[b])
                    e.wait_ge(S["vk_d"], v[b])
                    e.scalar_tensor_tensor(kd[:, b, :], vk[:, b, D:D + HALF], SCALING, e3[:, b, :], ALU.mult, ALU.mult).then_inc(S["kd_d"], 1)
                for b in range(NB):
                    e.wait_ge(S["a_ps"], v[b])
                    e.tensor_tensor(am[:, b, :].rearrange("p (h i) -> p h i", h=H),
                                    pde[b][:, :].rearrange("p (h i) -> p h i", h=H),
                                    upto[:].unsqueeze(1).broadcast_to([P, H, P]), ALU.mult).then_inc(S["am_d"], 1)
                for b in range(NB):
                    e.wait_ge(S["so_ps"], v[b])
                    e.tensor_reduce(hsum[:, b, :], pc[b][:, 0:D].rearrange("p (h v) -> p h v", h=H), AX.X, ALU.add).then_inc(S["hsum_d"], 1)
                    e.tensor_tensor(su[:, b, :], pc[b][:, D:2 * D], head_block[:], ALU.mult).then_inc(S["su_d"], 1)
                    e.wait_ge(S["hsum_d"], v[b])
                    e.tensor_scalar(hmean[:, b, :], hsum[:, b, :], 1.0 / DV, None, ALU.mult).then_inc(S["hmean_d"], 1)
                    e.wait_ge(S["su_d"], v[b])
                    e.scalar_tensor_tensor(st[:, b, :], st[:, b, :], e1[:, b, P - 1:P], su[:, b, :], ALU.mult, ALU.add).then_inc(S["st_d"], 1)
                    e.wait_ge(S["hmean_d"], v[b])
                    e.tensor_tensor(oc[:, b, :].rearrange("p (h v) -> p h v", h=H), pc[b][:, 0:D].rearrange("p (h v) -> p h v", h=H),
                                    hmean[:, b, :].unsqueeze(2).broadcast_to([P, H, DV]), ALU.subtract).then_inc(S["oc_d"], 1)
                hv = [hvar[:, b, :] for b in range(NB)]
                for b in range(NB):
                    e.wait_ge(S["osq_d"], v[b])
                    e.tensor_reduce(hvar[:, b, :], osq[:, b, :].rearrange("p (h v) -> p h v", h=H), AX.X, ALU.add).then_inc(S["hvar_d"], 1)
                    e.wait_ge(S["hvar_d"], v[b])
                    e.tensor_scalar(hvar[:, b, :], hvar[:, b, :], 1.0 / DV, EPS, ALU.mult, ALU.add).then_inc(S["hvs_d"], 1)
                for b in range(NB):
                    e.wait_ge(S["hrs_d"], v[b])
                    e.tensor_tensor(on[:, b, :].rearrange("p (h v) -> p h v", h=H), oc[:, b, :].rearrange("p (h v) -> p h v", h=H),
                                    hrs[:, b, :].unsqueeze(2).broadcast_to([P, H, DV]), ALU.mult).then_inc(S["on_d"], 1)
                    e.wait_ge(S["on_d"], v[b])
                    e.tensor_tensor(og[:, b, :], on[:, b, :], sg[:, b, :], ALU.mult).then_inc(S["og_d"], 1)
                for b in range(NB):
                    e.wait_ge(S[f"x2_st{b}"], 16 * n + 16)
                    e.wait_ge(S["y_ps"], v[b])
                    e.scalar_tensor_tensor(x2[:, b, :], pc[b][:, 0:D], 1.0, xt[b], ALU.mult, ALU.add, accum_out=sum2[:, b, :]).then_inc(S["x2_d"], 1)
                    e.wait_ge(S["x2_d"], v[b])
                    e.tensor_scalar(negmean2[:, b, :], sum2[:, b, :], -1.0 / D, None, ALU.mult).then_inc(S["mean2_d"], 1)
                for b in range(NB):
                    e.wait_ge(S["ssq2_d"], v[b])
                    e.tensor_scalar(vare2[:, b, :], ssq2[:, b, :], 1.0 / D, EPS, ALU.mult, ALU.add).then_inc(S["vare2_d"], 1)
                for b in range(NB):
                    e.wait_ge(S[f"xn_st{b}"], 16 * n + 16)
                    e.wait_ge(S["rstd2_d"], v[b])
                    e.tensor_scalar(x2n[:, b, :], x2[:, b, :], negmean2[:, b, :], rstd2[:, b, :], ALU.add, ALU.mult).then_inc(S["x2n_d"], 1)
                for b in range(NB):
                    e.wait_ge(S["lg_ps"], v[b])
                    e.tensor_copy(logits[:, b, bass.ds(n * E, E)], pc[b][:, D:D + E]).then_inc(S["lg_d"], 1)
            lg4 = logits[:].rearrange("p b (n c) -> p (b n) c", c=E)
            wide = lambda ap: ap.unsqueeze(2).broadcast_to([P, NT, E])
            e.wait_ge(S["lg_d"], NT)
            e.tensor_reduce(lmax[:], lg4, AX.X, ALU.max).then_inc(S["lmax_d"], 1)
            e.wait_ge(S["lmax_d"], 1)
            e.tensor_tensor(shifted[:], lg4, wide(lmax[:]), ALU.subtract).then_inc(S["shift_d"], 1)
            e.wait_ge(S["expo_d"], 1)
            e.tensor_reduce(lsum[:], expo[:], AX.X, ALU.add).then_inc(S["lsum_d"], 1)
            e.wait_ge(S["lsum_d"], 1)
            e.reciprocal(lrec[:], lsum[:]).then_inc(S["lrec_d"], 1)
            e.wait_ge(S["lrec_d"], 1)
            e.tensor_tensor(probs[:], expo[:], wide(lrec[:]), ALU.mult).then_inc(S["probs_d"], 1)
            e.wait_ge(S["probs_d"], 1)
            e.wait_ge(S["moe_c"], 9)
            mine = probs[:].unsqueeze(3).broadcast_to([P, NT, E, E])
            other = probs[:].unsqueeze(2).broadcast_to([P, NT, E, E])
            e.tensor_tensor(pq[:], other, mine, ALU.is_equal).then_inc(S["rank_d"], 1)
            e.tensor_tensor(pg[:], other, mine, ALU.is_gt).then_inc(S["rank_d"], 1)
            e.wait_ge(S["rank_d"], 1)
            e.tensor_tensor(pq[:], pq[:], earlier[:].unsqueeze(1).broadcast_to([P, NT, E, E]), ALU.mult).then_inc(S["rank_d"], 1)
            e.wait_ge(S["rank_d"], 3)
            e.tensor_tensor(pg[:], pg[:], pq[:], ALU.add).then_inc(S["rank_d"], 1)
            e.wait_ge(S["rank_d"], 4)
            e.tensor_tensor(pg[:], pg[:], other, ALU.mult).then_inc(S["rank_d"], 1)
            e.wait_ge(S["rank_d"], 5)
            e.tensor_reduce(before[:], pg[:], AX.X, ALU.add).then_inc(S["before_d"], 1)
            e.wait_ge(S["before_d"], 1)
            e.tensor_scalar(keep[:].rearrange("p c t -> p t c"), before[:], TOP_P, None, ALU.is_le).then_inc(S["keep_d"], 1)
            e.scalar_tensor_tensor(wts[:], before[:], TOP_P, probs[:], ALU.is_le, ALU.mult).then_inc(S["wts_d"], 1)
            e.wait_ge(S["pos_ps"], 1)
            e.tensor_copy(tot[:], pTot.rearrange("p (c t) -> p c t", c=E)).then_inc(S["tot_d"], 1)
            e.wait_ge(S["tot_d"], 1)
            src, k, cnt = tot, 1, 0
            while k < NT:
                dst = scan[cnt % 2]
                e.tensor_tensor(dst[:, :, k:], src[:, :, k:], src[:, :, :NT - k], ALU.add).then_inc(S["scan_d"], 1)
                e.tensor_copy(dst[:, :, :k], src[:, :, :k]).then_inc(S["scan_d"], 1)
                cnt += 1
                e.wait_ge(S["scan_d"], 2 * cnt)
                src, k = dst, 2 * k
            other_scan = scan[cnt % 2]
            e.tensor_tensor(other_scan[:], src[:], tot[:], ALU.subtract).then_inc(S["slot_d"], 1)
            e.tensor_scalar(tiles_i[:], src[:, :, NT - 1], float(P - 1), None, ALU.add).then_inc(S["slot_d"], 1)
            e.wait_ge(S["slot_d"], 2)
            e.tensor_tensor(slot[:], pPos.rearrange("p (c t) -> p c t", c=E), other_scan[:], ALU.add).then_inc(S["slot_d"], 1)
            e.tensor_scalar(tiles_s[:], tiles_i[:], 7, None, ALU.arith_shift_right).then_inc(S["slot_d"], 1)
            e.wait_ge(S["slot_d"], 4)
            e.scalar_tensor_tensor(slot[:], keep[:], -float(4 * TOK), slot[:], ALU.mult, ALU.add).then_inc(S["slot_d"], 1)
            e.tensor_scalar(tiles_f[0][:], tiles_s[:], float(MINT), None, ALU.max).then_inc(S["slot_d"], 1)
            e.wait_ge(S["slot_d"], 6)
            e.tensor_scalar(slot_i[:], slot[:], float(4 * TOK), None, ALU.add).then_inc(S["sloti_d"], 1)
            src, k, cnt2 = tiles_f[0], 1, 0
            while k < E:
                dst = tiles_f[(cnt2 + 1) % 2]
                e.tensor_tensor(dst[:, k:], src[:, k:], src[:, :E - k], ALU.add).then_inc(S["scan_d"], 1)
                e.tensor_copy(dst[:, :k], src[:, :k]).then_inc(S["scan_d"], 1)
                cnt2 += 1
                e.wait_ge(S["scan_d"], 2 * (cnt + cnt2))
                src, k = dst, 2 * k
            e.memset(starts[:, 0:1], 0).then_inc(S["starts_d"], 1)
            e.tensor_copy(starts[:, 1:E + 1], src[:]).then_inc(S["starts_d"], 1)
            e.wait_ge(S["starts_d"], 2)
            e.wait_ge(S["sloti_d"], 1)
            e.tensor_scalar(sb_i[:], slot_i[:], P - 1, None, ALU.bitwise_and).then_inc(S["slotba_d"], 1)
            e.tensor_scalar(sa_i[:], slot_i[:], 7, None, ALU.arith_shift_right).then_inc(S["slotba_d"], 1)
            e.wait_ge(S["slotba_d"], 2)
            e.tensor_copy(slot_b[:], sb_i[:].rearrange("p c t -> p (c t)")).then_inc(S["slotf_d"], 1)
            e.tensor_copy(slot_a[:], sa_i[:]).then_inc(S["slotf_d"], 1)
            e.wait_ge(S["slotf_d"], 2)
            e.tensor_tensor(hot_a[:], slot_a[:].rearrange("p c t -> p (c t)").unsqueeze(2).broadcast_to([P, E * NT, NT]),
                            iota_a[:].unsqueeze(1).broadcast_to([P, E * NT, NT]), ALU.is_equal).then_inc(S["hota_d"], 1)
            e.wait_ge(S["hota_d"], 1)
            e.tensor_tensor(id_a[:].rearrange("p (c t a) -> p c t a", c=E, t=NT), hot_a[:].rearrange("p (c t) a -> p c t a", c=E),
                            tok_id[:].unsqueeze(1).unsqueeze(3).broadcast_to([P, E, NT, NT]), ALU.mult).then_inc(S["ida_d"], 1)
            with e.Fori(0, E) as ei:
                for t in range(NT):
                    last = e.tensor_scalar(hot_b[:, bass.ds(ei * NT * P + t * P, P)], iota_b[:], slot_b[:, bass.ds(ei * NT + t, 1)], None, ALU.is_equal)
                last.then_inc(S["hotb_d"], 1)
            e.wait_ge(S["list_ps"], E)
            e.tensor_scalar(empty[:], pList[:, 0:E * NT], 0.0, dummy[:], ALU.is_equal, ALU.mult).then_inc(S["empty_d"], 1)
            e.wait_ge(S["empty_d"], 1)
            e.scalar_tensor_tensor(lists[:], pList[:, 0:E * NT], -1.0, empty[:], ALU.add, ALU.add).then_inc(S["lists_d"], 1)

            def vec_x(i):
                e.wait_ge(S["xhi_d"], i + 1)
                e.tensor_tensor(xlo[:], pXT[:, 0:KD * P], xhi[:].bitcast(F32), ALU.subtract).then_inc(S["xlo_d"], 1)
                e.tensor_copy(wcur[:], xg[:, D:ROW]).then_inc(S["wcur_d"], 1)

            def vec_ht(i):
                e.wait_ge(S["hhi_d"], i)
                e.tensor_tensor(hlo[:], pHT[:], hhi[:].bitcast(F32), ALU.subtract).then_inc(S["hlo_d"], 1)

            def vec_tile(ei, i, first):
                if not first:
                    vec_ht(i)
                e.wait_ge(S["wcur_d"], i + 2)
                e.wait_ge(S["sg_done"], i + 1)
                e.wait_ge(S["u_ps"], i + 1)
                e.scalar_tensor_tensor(hid[:], gact[:], wcur[:, bass.ds(ei, 1)], pU[:], ALU.mult, ALU.mult).then_inc(S["hid_d"], 1)
                e.wait_ge(S["hid_d"], i + 1)
                vec_x(i + 1)

            def vec_pair(pr, first, more):
                for q in range(2):
                    ei = 2 * pr + q
                    t0 = e.value_load(starts[0:1, bass.ds(ei, 1)], min_val=0, max_val=NT * E) if not (first and q == 0) else 0
                    t1 = e.value_load(starts[0:1, bass.ds(ei + 1, 1)], min_val=MINT, max_val=NT * E)
                    vec_tile(ei, t0, first and q == 0)
                    if more or q == 0:
                        split_lo(ei + 1, 1 - q)
                    with e.Fori(t0 + 1, t1) as i:
                        vec_tile(ei, i, False)
            vec_x(0)
            vec_pair(0, True, True)
            with e.Fori(1, E // 2 - 1) as pr:
                vec_pair(pr, False, True)
            vec_pair(E // 2 - 1, False, False)
            n_tiles = e.value_load(starts[0:1, E:E + 1], min_val=MINT * E, max_val=NT * E)
            vec_ht(n_tiles)

        @block.tensor
        def _(e):
            def proj(dst, lhs, rhs, done=None):
                for k in range(KD):
                    last = e.matmul(dst, lhs(k), rhs(k), start=(k == 0), stop=(k == KD - 1))
                return last
            for s in ("w_q", "w_k", "w_kg1", "w_v", "w_g", "w_o", "w_r"):
                e.wait_ge(S[s], 16)
            e.wait_ge(S["w_kg2"], 48)
            e.wait_ge(S["const"], 8)
            with e.Fori(0, NCH) as n:
                v = [2 * n + (b + 1) for b in range(NB)]
                for b in range(NB):
                    e.wait_ge(S["xn_d"], v[b])
                    for k in range(KD):
                        last = e.transpose(pa[b][:, k * P:(k + 1) * P], xn[:, b, k * P:(k + 1) * P], ident[:])
                    last.then_inc(S["xnT_ps"], 1)
                for b in range(NB):
                    xT = lambda k: xnT[:, b, k * P:(k + 1) * P]
                    e.wait_ge(S["xnT_d"], v[b])
                    proj(pa[b][0:R, 0:P], lambda k: wkg1[:, k, :], xT)
                    proj(pa[b][:, 256:256 + P], lambda k: wq[:, k, :], xT)
                    proj(pa[b][:, 256 + P:512], lambda k: wk[:, k, :], xT).then_inc(S["qkg_ps"], 1)
                    proj(pc[b][:, 0:D], xT, lambda k: wv[:, k, :])
                    proj(pc[b][:, D:D + HALF], xT, lambda k: wk[:, k, :]).then_inc(S["vk_ps"], 1)
                for b in range(NB):
                    xT = lambda k: xnT[:, b, k * P:(k + 1) * P]
                    e.wait_ge(S["g1T_d"], v[b])
                    e.matmul(pde[b][:, 0:HALF], g1T[:, b, :], wkg2[:], start=True, stop=False)
                    e.matmul(pde[b][:, 0:HALF], ones_row[:], bkg2_row[:], start=False, stop=True)
                    e.matmul(pde[b][:, HALF:HALF + D], ones_row[:], bg_row[:], start=True, stop=False)
                    e.matmul(pde[b][:, HALF:HALF + D], xT(0), wg[:, 0, :], start=False, stop=False)
                    e.matmul(pde[b][:, HALF:HALF + D], xT(1), wg[:, 1, :], start=False, stop=True).then_inc(S["zg_ps"], 1)
                for b in range(NB):
                    e.wait_ge(S["gneg_d"], v[b])
                    e.matmul(pde[b][:, 512:512 + P], gneg[:, b, :], upto[:], start=True, stop=True)
                    e.matmul(pde[b][:, 512 + P:512 + P + HALF], after[:], gneg[:, b, :], start=True, stop=True).then_inc(S["cum_ps"], 1)
                for b in range(NB):
                    e.wait_ge(S["qm_d"], v[b])
                    e.wait_ge(S["kn_d"], v[b])
                    e.wait_ge(S["e3_d"], v[b])
                    e.wait_ge(S["gs_d"], v[b])
                    for j in range(2):
                        last = e.matmul(pde[b][:, j * 512:(j + 1) * 512], kn[:, b, :], qm[:, b, j * 512:(j + 1) * 512], start=True, stop=True)
                    last.then_inc(S["a_ps"], 1)
                for b in range(NB):
                    e.wait_ge(S["kd_d"], v[b])
                    e.wait_ge(S["vk_d"], v[b])
                    e.matmul(pc[b][:, D:2 * D], kd[:, b, :], vk[:, b, 0:D], start=True, stop=True)
                    e.wait_ge(S["am_d"], v[b])
                    e.matmul(pc[b][:, 0:D], qd[:, b, :], st[:, b, :], start=True, stop=False, skip_group_check=True)
                    for h in range(H):
                        last = e.matmul(pc[b][:, h * DV:(h + 1) * DV], am[:, b, h * P:(h + 1) * P], vk[:, b, h * DV:(h + 1) * DV],
                                        start=False, stop=(h == H - 1), skip_group_check=True)
                    last.then_inc(S["so_ps"], 1)
                for b in range(NB):
                    e.wait_ge(S["og_d"], v[b])
                    for k in range(KD):
                        last = e.transpose(pa[b][:, k * P:(k + 1) * P], og[:, b, k * P:(k + 1) * P], ident[:])
                    last.then_inc(S["ogT_ps"], 1)
                for b in range(NB):
                    e.wait_ge(S["ogT_d"], v[b])
                    proj(pc[b][:, 0:D], lambda k: ogT[:, b, k * P:(k + 1) * P], lambda k: wo[:, k, :]).then_inc(S["y_ps"], 1)
                for b in range(NB):
                    e.wait_ge(S["x2n_d"], v[b])
                    for k in range(KD):
                        last = e.transpose(pa[b][:, k * P:(k + 1) * P], x2n[:, b, k * P:(k + 1) * P], ident[:])
                    last.then_inc(S["x2nT_ps"], 1)
                for b in range(NB):
                    e.wait_ge(S["x2nT_d"], v[b])
                    proj(pc[b][:, D:D + E], lambda k: x2nT[:, b, k * P:(k + 1) * P], lambda k: rw_sb[:, k, :]).then_inc(S["lg_ps"], 1)
            e.wait_ge(S["moe_c"], 9)
            e.wait_ge(S["keep_d"], 1)
            kp = keep[:].rearrange("p c t -> p (c t)")
            e.matmul(pPos, tril[:], kp, start=True, stop=True)
            e.matmul(pTot, ones[:], kp, start=True, stop=True).then_inc(S["pos_ps"], 1)
            e.wait_ge(S["ida_d"], 1)
            with e.Fori(0, E) as ei:
                e.wait_ge(S["hotb_d"], ei + 1)
                for t in range(NT):
                    last = e.matmul(pList[:, bass.ds(ei * NT, NT)], hot_b[:, bass.ds(ei * NT * P + t * P, P)],
                                    id_a[:, bass.ds(ei * NT * NT + t * NT, NT)], start=(t == 0), stop=(t == NT - 1))
                last.then_inc(S["list_ps"], 1)

            def products(dst, parts, n, done):
                last = None
                for m, (a, w) in enumerate(parts):
                    last = e.matmul(dst, a, w, start=(m == 0), stop=(m == len(parts) - 1))
                last.then_inc(S[done], 1)

            def x_parts(q, m):
                for k in range(KD):
                    c = slice(k * P, (k + 1) * P)
                    w = slice(m * WN + k * I, m * WN + (k + 1) * I)
                    yield xhi[:, c], whi[q][:, w]
                    yield xhi[:, c], wlo[q][:, w]
                    yield xlo[:, c], whi[q][:, w]

            def h_parts(q):
                for k in range(IC):
                    c = slice(k * P, (k + 1) * P)
                    w = slice(2 * WN + k * D, 2 * WN + (k + 1) * D)
                    yield hhi[:, c], whi[q][:, w]
                    yield hhi[:, c], wlo[q][:, w]
                    yield hlo[:, c], whi[q][:, w]

            def turn_x(i):
                e.wait_ge(S["gath"], 16 * i + 16)
                for k in range(KD):
                    last = e.transpose(pXT[:, k * P:(k + 1) * P], xg[:, k * P:(k + 1) * P], ident[:])
                last.then_inc(S["x_ps"], 1)

            def turn_h(i):
                e.wait_ge(S["hid_d"], i)
                for k in range(IC):
                    last = e.transpose(pHT[:, k * P:(k + 1) * P], hid[:, k * P:(k + 1) * P], ident[:])
                last.then_inc(S["ht_ps"], 1)

            def down(i, q):
                e.wait_ge(S["hlo_d"], i)
                e.wait_ge(S["yev"], i + 1)
                products(pY[:, 0:D], list(h_parts(q)), D, "yps")

            def pe_tile(i, q, q_before, first):
                e.wait_ge(S["xlo_d"], i + 1)
                if not first:
                    e.wait_ge(S["sg_done"], i)
                products(pG, list(x_parts(q, 0)), I, "g_ps")
                if not first:
                    turn_h(i)
                products(pU, list(x_parts(q, 1)), I, "u_ps")
                turn_x(i + 1)
                if not first:
                    down(i, q_before)

            def pe_pair(pr, first):
                for q in range(2):
                    ei = 2 * pr + q
                    t0 = e.value_load(starts[0:1, bass.ds(ei, 1)], min_val=0, max_val=NT * E) if not (first and q == 0) else 0
                    t1 = e.value_load(starts[0:1, bass.ds(ei + 1, 1)], min_val=MINT, max_val=NT * E)
                    e.wait_ge(S["wlo_d"], 3 * ei + 3)
                    pe_tile(t0, q, 1 - q, first and q == 0)
                    with e.Fori(t0 + 1, t1) as i:
                        pe_tile(i, q, q, False)
            e.wait_ge(S["starts_d"], 2)
            turn_x(0)
            pe_pair(0, True)
            with e.Fori(1, E // 2) as pr:
                pe_pair(pr, False)
            n_tiles = e.value_load(starts[0:1, E:E + 1], min_val=MINT * E, max_val=NT * E)
            turn_h(n_tiles)
            down(n_tiles, 1)


_INS = ['L0_attn_x', 'L0_attn_Wq', 'L0_attn_Wk', 'L0_attn_Wkg1', 'L0_attn_Wkg2', 'L0_attn_bkg2', 'L0_attn_Wv', 'L0_attn_Wg',
        'L0_attn_bg', 'L0_attn_Wo', 'L0_ffn_router_w', 'L0_ffn_gate_w', 'L0_ffn_up_w', 'L0_ffn_down_w']


def kernel(**inputs):
    import numpy as _np
    import concourse.bacc as _bacc
    from concourse import mybir as _mybir
    from concourse.bass_utils import run_bass_kernel_spmd as _run

    nc = _bacc.Bacc("TRN2", target_bir_lowering=False, num_devices=1)
    arrays, args = {}, []
    for name in _INS:
        a = inputs[name]
        if name.startswith("L0_ffn"):
            a = _np.swapaxes(a, -1, -2)
        a = _np.ascontiguousarray(a)
        arrays[f"in_{name}_dram"] = a
        args.append(nc.dram_tensor(f"in_{name}_dram", a.shape, _mybir.dt.from_np(a.dtype), kind="ExternalInput").ap())
    args.append(nc.dram_tensor("out_0_dram", (2, 1024, 256), _mybir.dt.float32, kind="ExternalOutput").ap())
    gla_moe_layer(nc, *args)
    r = _run(nc, [arrays], core_ids=[0])
    return r.results[0]["out_0_dram"]
```

```python
import concourse.bass as bass
from concourse import mybir
from contextlib import ExitStack


def gla_moe_layer(nc, x, Wq, Wk, Wkg1, Wkg2, bkg2, Wv, Wg, bg, Wo, rw, gate_w, up_w, down_w, out):
    F32 = mybir.dt.float32
    ALU = mybir.AluOpType
    ACT = mybir.ActivationFunctionType
    AX = mybir.AxisListType
    P = 128
    NB, T, D = 2, 1024, 256
    NCH = T // P
    H = 8
    DK, DV = 128 // H, D // H
    HALF = D // 2
    KD = D // P
    R = 16
    E = 8
    SCALING = float(DV) ** -0.5
    GK = 1.0 / 16.0
    EPS = 1e-5
    TOP_P = 0.9
    F32R = mybir.dt.float32r
    F16 = mybir.dt.float16
    I32 = mybir.dt.int32
    U32 = mybir.dt.uint32
    NT = NB * NCH
    TOK = NB * T
    I = 512
    IC = I // P
    WN = KD * I
    ROW = D + E
    SPLIT = 3
    MINT = SPLIT + 1
    LAG = 4

    rows = nc.dram_tensor("token_rows", (TOK + P, ROW), F32, kind="Internal").ap()
    acc = nc.dram_tensor("token_sums", (TOK + P, D), F32, kind="Internal").ap()

    with ExitStack() as ctx:
        def sb(name, shape, dt=F32):
            return ctx.enter_context(nc.sbuf_tensor(name, shape, dt))

        def sem(name):
            return ctx.enter_context(nc.semaphore(name))

        xs = sb("xs", [P, NB, NCH * D])
        wq = sb("wq", [P, KD, HALF]); wk = sb("wk", [P, KD, HALF])
        wv = sb("wv", [P, KD, D]); wg = sb("wg", [P, KD, D]); wo = sb("wo", [P, KD, D])
        wkg1 = sb("wkg1", [P, KD, R]); wkg2 = sb("wkg2", [R + 1, HALF + D])
        rw_sb = sb("rw_sb", [P, KD, E])
        ident = sb("ident", [P, P]); upto = sb("upto", [P, P]); after = sb("after", [P, P])
        head_rows = sb("head_rows", [P, H]); head_block = sb("head_block", [P, D])
        stats = sb("stats", [P, NB, 6 * NCH]); mv = sb("mv", [P, NB, NCH, 2]); vare = sb("vare", [P, NB, NCH]); rstd = sb("rstd", [P, NB, NCH])
        x2 = sb("x2", [P, NB, D]); sum2 = sb("sum2", [P, NB, 1]); negmean2 = sb("negmean2", [P, NB, 1]); ssq2 = sb("ssq2", [P, NB, 1]); sq2 = sb("sq2", [P, NB, D]); vare2 = sb("vare2", [P, NB, 1]); rstd2 = sb("rstd2", [P, NB, 1])
        minus_half = sb("minus_half", [P, 2 * NCH]); eps_col = sb("eps_col", [P, 1])
        xn = sb("xn", [P, NB, D]); xnT = sb("xnT", [P, NB, KD * P])
        g1T = sb("g1T", [R + 1, NB, P]); qkT = sb("qkT", [P, NB, 2 * P])
        vk = sb("vk", [P, NB, D + HALF])
        work = sb("work", [P, NB * (2 * H * P + 9 * D)])
        taken = [0]

        def part(width):
            at = taken[0]
            taken[0] += NB * width
            return work[:, at:at + NB * width].rearrange("p (b n) -> p b n", b=NB)
        gs = part(D); sg = part(D); sgm = part(D); zl = part(HALF + D); zr = part(HALF + D)
        e1 = sb("e1", [P, NB, P]); e2 = sb("e2", [P, NB, P]); e3 = sb("e3", [P, NB, HALF])
        qd = sb("qd", [P, NB, P]); kn = sb("kn", [P, NB, P]); kd = sb("kd", [P, NB, HALF])
        qm = part(H * P); am = part(H * P)
        st = sb("st", [P, NB, D]); su = sb("su", [P, NB, D])
        hsum = sb("hsum", [P, NB, H]); hmean = sb("hmean", [P, NB, H])
        oc = part(D); osq = part(D); on = part(D)
        hvar = sb("hvar", [P, NB, H]); hrs = sb("hrs", [P, NB, H])
        og = sb("og", [P, NB, D]); ogT = sb("ogT", [P, NB, KD * P])
        x2n = sb("x2n", [P, NB, D]); x2nT = sb("x2nT", [P, NB, KD * P])
        logits = sb("logits", [P, NB, NCH * E])

        pe8 = lambda name, dt=F32: sb(name, [P, NT, E], dt)
        probs = pe8("probs"); expo = pe8("expo"); lmax = sb("lmax", [P, NT]); lsum = sb("lsum", [P, NT]); lrec = sb("lrec", [P, NT])
        shifted = pe8("shifted"); wts = pe8("wts"); before = sb("before", [P, NT, E]); 
        pg = sb("pg", [P, NT, E, E]); pq = sb("pq", [P, NT, E, E]); earlier = sb("earlier", [P, E, E])
        keep = sb("keep", [P, E, NT]); tot = sb("tot", [P, E, NT]); scan = [sb(f"scan{i}", [P, E, NT]) for i in range(2)]
        slot = sb("slot", [P, E, NT]); slot_i = sb("slot_i", [P, E, NT], I32); sb_i = sb("sb_i", [P, E, NT], I32); sa_i = sb("sa_i", [P, E, NT], I32)
        slot_b = sb("slot_b", [P, E * NT], F16); slot_a = sb("slot_a", [P, E * NT])
        tril = sb("tril", [P, P]); ones = sb("ones", [P, P])
        iota_b = sb("iota_b", [P, P], F16); iota_a = sb("iota_a", [P, NT]); tok_id = sb("tok_id", [P, NT]); dummy = sb("dummy_row", [P, 1])
        hot_a = sb("hot_a", [P, NT, NT]); id_a = sb("id_a", [P, NT, NT], F16); hot_b = work[:, 0:NT * P // 2].bitcast(F16)
        empty = sb("empty", [P, NT])
        tiles_i = sb("tiles_i", [P, E], I32); tiles_s = sb("tiles_s", [P, E], I32); tiles_f = [sb(f"tiles_f{i}", [P, E]) for i in range(2)]
        starts = sb("starts", [P, E + 1], I32)
        zrow = sb("zrow", [P, ROW])
        raw = sb("raw", [P, 3 * WN])
        whi = [sb(f"whi{q}", [P, 3 * WN], F32R) for q in range(2)]; wlo = [sb(f"wlo{q}", [P, 3 * WN], F32R) for q in range(2)]
        flat = sb("flat", [P, E * NT + NT + 2 * LAG], U32); idx_g = [sb(f"idx_g{u}", [P, 1], U32) for u in range(2)]; idx_s = [sb(f"idx_s{u}", [P, 1], U32) for u in range(2)]
        xg = sb("xg", [P, 2 * ROW]); xcur = sb("xcur", [P, ROW]); wcur = sb("wcur", [P, E])
        xhi = sb("xhi", [P, KD * P], F32R); xlo = sb("xlo", [P, KD * P], F32R)
        gact = sb("gact", [P, I]); hid = sb("hid", [P, I]); hhi = sb("hhi", [P, I], F32R); hlo = sb("hlo", [P, I], F32R)
        ybuf = sb("ybuf", [P, 2 * D])

        pa = [ctx.enter_context(nc.psum_tensor(f"pa{b}", [P, 512], F32)) for b in range(NB)]
        pc = [ctx.enter_context(nc.psum_tensor(f"pc{b}", [P, 512], F32)) for b in range(NB)]
        py = [ctx.enter_context(nc.psum_tensor(f"py{b}", [P, 512], F32)) for b in range(NB)]
        pA = ctx.enter_context(nc.psum_tensor("pA", [P, 1024], F32))

        S = {}
        for name in ("x_in w_q w_k w_kg1 w_kg2 wkg2_z w_v w_g w_o w_r const memz "
                     "stats_d mv_d vare_d vare2_d rstd_d xn_d xnT_ps xnT_d qkg_ps g1T_d qkT_d vk_ps vk_d "
                     "zg_ps za_d zr_d ze_d zl_d gneg_d gs_d sgm_d sg_d cum_ps e1_d e2_d e3_d "
                     "qd_d kn_d kd_d qm_d a_ps am_d so_ps su_d st_d hsum_d hmean_d oc_d osq_d hvar_d hvs_d hrs_d "
                     "on_d og_d ogT_ps ogT_d y_ps x2_d x2_st0 x2_st1 mean2_d ssq2_d rstd2_d x2n_d x2nT_ps x2nT_d lg_ps lg_d out_st "
                     "lmax_d shift_d expo_d lsum_d lrec_d probs_d rank_d before_d wts_d keep_d w_st rows_z pos_ps tot_d scan_d slot_d "
                     "sloti_d slotba_d slotf_d hota_d ida_d hotb_d list_ps empty_d lists_d starts_d xn_st0 xn_st1 "
                     "raw_in whi_d wlo_d gath0 gath1 flat_d idxg_d idxs_d x_ps xhi_d xlo_d wcur_d take_d g_ps sg_done u_ps hid_d ht_ps hhi_d hlo_d yps yev scat moe_c moe_z pass_ pass_v").split():
            S[name] = sem(name)
        block = ctx.enter_context(nc.Block())

        pG = pA[:, 0:I]; pU = pA[:, I:2 * I]; pXT = pa[0]; pHT = pa[1]; pY = pc[0]
        pPos = py[0][:, 0:P]; pTot = py[1][:, 0:P]; pList = pc[1][:, 0:NT]

        @block.sync
        def _(e):
            for b in range(NB):
                for hf in range(2):
                    e.dma_start(xs[:, b, hf * 1024:(hf + 1) * 1024].rearrange("p (n d) -> p n d", d=D),
                                x[b, hf * 512:(hf + 1) * 512].rearrange("(n p) d -> p n d", p=P)).then_inc(S["x_in"], 16)
            def load_expert(ei):
                for m, w in enumerate((gate_w, up_w, down_w)):
                    e.dma_start(raw[:, m * WN:(m + 1) * WN].rearrange("p (c n) -> p c n", c=w.shape[1] // P),
                                w[bass.ds(ei, 1)].rearrange("a (c p) n -> p (a c) n", p=P)).then_inc(S["raw_in"], 16)
            load_expert(0)
            e.wait_ge(S["moe_z"], 1)
            e.dma_start(rows[TOK:TOK + P, :], zrow[:]).then_inc(S["rows_z"], 16)
            e.dma_start(acc[TOK:TOK + P, :], zrow[:, 0:D]).then_inc(S["rows_z"], 16)
            for b in range(NB):
                e.sem_inc(S[f"x2_st{b}"], 16)
                e.sem_inc(S[f"xn_st{b}"], 16)
            with e.Fori(0, NCH) as n:
                for b in range(NB):
                    r0 = b * T + n * P
                    e.wait_ge(S["x2_d"], 2 * n + (b + 1))
                    e.dma_start(acc[bass.ds(r0, P), :], x2[:, b, :]).then_inc(S[f"x2_st{b}"], 16)
                for b in range(NB):
                    r0 = b * T + n * P
                    e.wait_ge(S["x2n_d"], 2 * n + (b + 1))
                    e.dma_start(rows[bass.ds(r0, P), 0:D], x2n[:, b, :]).then_inc(S[f"xn_st{b}"], 16)
            e.wait_ge(S["wts_d"], 1)
            e.dma_start(rows[0:TOK, D:ROW].rearrange("(t p) c -> p t c", p=P), wts[:]).then_inc(S["w_st"], 16)
            with e.Fori(1, E) as ei:
                e.wait_ge(S["wlo_d"], 3 * ei)
                load_expert(ei)
            e.wait_ge(S["starts_d"], 2)
            n_tiles = e.value_load(starts[0:1, E:E + 1], min_val=MINT * E, max_val=NT * E)
            e.wait_ge(S["scat"], ((n_tiles + LAG + 1) // 2) * 32)
            e.dma_start(out.rearrange("b t d -> (b t) d"), acc[0:TOK, :]).then_inc(S["out_st"], 16)
            e.wait_ge(S["out_st"], 16)

        @block.gpsimd
        def _(e):
            e.memset(g1T[:], 1.0).then_inc(S["const"], 1)
            e.memset(wkg2[:], 0.0).then_inc(S["wkg2_z"], 1)
            e.memset(minus_half[:], -0.5).then_inc(S["const"], 1)
            e.memset(eps_col[:], EPS).then_inc(S["const"], 1)
            e.memset(ident[:], 0.0).then_inc(S["memz"], 1)
            e.memset(upto[:], 1.0).then_inc(S["memz"], 1)
            e.memset(after[:], 1.0).then_inc(S["memz"], 1)
            e.memset(head_rows[:], 1.0).then_inc(S["memz"], 1)
            e.memset(head_block[:], 1.0).then_inc(S["memz"], 1)
            e.memset(st[:], 0.0).then_inc(S["const"], 1)
            e.memset(zrow[:], 0.0).then_inc(S["moe_z"], 1)
            e.memset(ybuf[:], 0.0).then_inc(S["moe_c"], 1)
            e.memset(ones[:], 1.0).then_inc(S["moe_c"], 1)
            e.memset(tril[:], 1.0).then_inc(S["memz"], 1)
            e.memset(earlier[:], 1.0).then_inc(S["memz"], 1)
            e.iota(iota_b[:], pattern=[[1, P]], base=0, channel_multiplier=0, allow_small_or_imprecise_dtypes=True).then_inc(S["moe_c"], 1)
            e.iota(iota_a[:], pattern=[[1, NT]], base=0, channel_multiplier=0, allow_small_or_imprecise_dtypes=True).then_inc(S["moe_c"], 1)
            e.iota(tok_id[:], pattern=[[P, NT]], base=1, channel_multiplier=1, allow_small_or_imprecise_dtypes=True).then_inc(S["moe_c"], 1)
            e.iota(dummy[:], pattern=[[1, 1]], base=TOK + 1, channel_multiplier=1, allow_small_or_imprecise_dtypes=True).then_inc(S["moe_c"], 1)
            e.iota(flat[:].bitcast(I32), pattern=[[0, E * NT + NT + 2 * LAG]], base=TOK, channel_multiplier=1).then_inc(S["moe_c"], 1)
            e.wait_ge(S["memz"], 7)
            e.affine_select(out=ident[:], in_=ident[:], compare_op=ALU.not_equal, fill=1.0, base=0,
                            pattern=[[-1, P]], channel_multiplier=1).then_inc(S["const"], 1)
            e.affine_select(out=upto[:], in_=upto[:], compare_op=ALU.is_ge, fill=0.0, base=0,
                            pattern=[[1, P]], channel_multiplier=-1).then_inc(S["const"], 1)
            e.affine_select(out=tril[:], in_=tril[:], compare_op=ALU.is_gt, fill=0.0, base=0,
                            pattern=[[1, P]], channel_multiplier=-1).then_inc(S["moe_c"], 1)
            e.affine_select(out=earlier[:], in_=earlier[:], compare_op=ALU.is_gt, fill=0.0, base=0,
                            pattern=[[1, E], [-1, E]], channel_multiplier=0).then_inc(S["moe_c"], 1)
            e.affine_select(out=after[:], in_=after[:], compare_op=ALU.is_gt, fill=0.0, base=0,
                            pattern=[[-1, P]], channel_multiplier=1).then_inc(S["const"], 1)
            e.affine_select(out=head_rows[:], in_=head_rows[:], compare_op=ALU.is_ge, fill=0.0, base=0,
                            pattern=[[-DK, H]], channel_multiplier=1).then_inc(S["memz"], 1)
            e.affine_select(out=head_block[:], in_=head_block[:], compare_op=ALU.is_ge, fill=0.0, base=0,
                            pattern=[[-DK, H], [0, DV]], channel_multiplier=1).then_inc(S["memz"], 1)
            e.wait_ge(S["memz"], 9)
            e.affine_select(out=head_rows[:], in_=head_rows[:], compare_op=ALU.is_ge, fill=0.0, base=DK - 1,
                            pattern=[[DK, H]], channel_multiplier=-1).then_inc(S["const"], 1)
            e.affine_select(out=head_block[:], in_=head_block[:], compare_op=ALU.is_ge, fill=0.0, base=DK - 1,
                            pattern=[[DK, H], [0, DV]], channel_multiplier=-1).then_inc(S["const"], 1)
            e.wait_ge(S["const"], 9)
            e.wait_ge(S["vare_d"], 1)
            e.tensor_tensor(rstd[:].rearrange("p b n -> p (b n)"), vare[:].rearrange("p b n -> p (b n)"), minus_half[:], ALU.pow).then_inc(S["rstd_d"], 1)
            def pool_step(n, attend, project, finish):
                v = [2 * n + (b + 1) for b in range(NB)]
                nxt = [2 * n + (b + 3) for b in range(NB)]
                prv = [2 * n + (b - 1) for b in range(NB)]
                if attend:
                    for b in range(NB):
                        e.wait_ge(S["oc_d"], v[b])
                        e.tensor_tensor(osq[:, b, :], oc[:, b, :], oc[:, b, :], ALU.mult).then_inc(S["osq_d"], 1)
                def spread_q(b):
                    e.wait_ge(S["qd_d"], nxt[b])
                    if attend:
                        e.wait_ge(S["a_ps"], v[b])
                    e.tensor_tensor(qm[:, b, :].rearrange("p (h i) -> p h i", h=H),
                                    qd[:, b, :].unsqueeze(1).broadcast_to([P, H, P]),
                                    head_rows[:].unsqueeze(2).broadcast_to([P, H, P]), ALU.mult).then_inc(S["qm_d"], 1)

                if project:
                    spread_q(0)
                    spread_q(1)
            pool_step(-1, False, True, False)
            pool_step(0, True, True, False)
            with e.Fori(1, NCH - 1) as n:
                pool_step(n, True, True, True)
            pool_step(NCH - 1, True, False, True)
            pool_step(NCH, False, False, True)

            e.wait_ge(S["moe_c"], 9)
            e.sem_inc(S["yev"], LAG)
            e.sem_inc(S["take_d"], 2)
            e.wait_ge(S["w_st"], 16)
            e.wait_ge(S["rows_z"], 32)
            for b in range(NB):
                e.wait_ge(S[f"x2_st{b}"], 16 * NCH + 16)
                e.wait_ge(S[f"xn_st{b}"], 16 * NCH + 16)
            e.wait_ge(S["lists_d"], 2)

            def gather(i, u):
                e.wait_ge(S["take_d"], i + 1)
                e.sem_inc(S["pass_"], 1)
                e.tensor_copy(idx_g[u][:], flat[:, bass.ds(i + LAG, 1)]).then_inc(S["idxg_d"], 1)
                e.wait_ge(S["idxg_d"], i + 1)
                e.sem_inc(S["pass_"], 1)
                e.indirect_dma_start(out=xg[:, u * ROW:(u + 1) * ROW], out_offset=None, in_=rows[:, :],
                                     in_offset=bass.IndirectOffsetOnAxis(ap=idx_g[u][:], axis=0)).then_inc(S[f"gath{u}"], 16)

            def scatter(i, u, first=False):
                e.wait_ge(S["yev"], i + 1)
                if not first:
                    e.wait_ge(S["scat"], 16 * i)
                e.sem_inc(S["pass_"], 1)
                e.tensor_copy(idx_s[u][:], flat[:, bass.ds(i, 1)]).then_inc(S["idxs_d"], 1)
                e.wait_ge(S["idxs_d"], i + 1)
                e.sem_inc(S["pass_"], 1)
                e.indirect_dma_start(out=acc[:, :], out_offset=bass.IndirectOffsetOnAxis(ap=idx_s[u][:], axis=0),
                                     in_=ybuf[:, u * D:(u + 1) * D], in_offset=None, compute_op=ALU.add).then_inc(S["scat"], 16)

            gather(0, 0)
            gather(1, 1)
            scatter(0, 0, first=True)
            scatter(1, 1)
            n_tiles = e.value_load(starts[0:1, E:E + 1], min_val=MINT * E, max_val=NT * E)
            with e.Fori(1, (n_tiles + LAG + 1) // 2) as j:
                for u in range(2):
                    gather(2 * j + u, u)
                    scatter(2 * j + u, u)

        @block.scalar
        def _(e):
            for dst, src, s in ((wq, Wq, "w_q"), (wk, Wk, "w_k"), (wkg1, Wkg1, "w_kg1"), (wv, Wv, "w_v"), (wg, Wg, "w_g"), (wo, Wo, "w_o"), (rw_sb, rw, "w_r")):
                e.dma_start(dst[:], src.rearrange("(k p) n -> p k n", p=P)).then_inc(S[s], 16)
            e.wait_ge(S["wkg2_z"], 1)
            e.dma_start(wkg2[0:R, 0:HALF], Wkg2).then_inc(S["w_kg2"], 16)
            e.dma_start(wkg2[R:R + 1, 0:HALF], bkg2.rearrange("(a n) -> a n", a=1)).then_inc(S["w_kg2"], 16)
            e.dma_start(wkg2[R:R + 1, HALF:HALF + D], bg.rearrange("(a n) -> a n", a=1)).then_inc(S["w_kg2"], 16)
            def split_hi(ei, q, m):
                e.wait_ge(S["raw_in"], 48 * ei + 48)
                e.activation(whi[q][:, m * WN:(m + 1) * WN], raw[:, m * WN:(m + 1) * WN], ACT.Copy).then_inc(S["whi_d"], 1)
            for m in range(SPLIT):
                split_hi(0, 0, m)
            e.preload_act_table_set("natural_log_exp_and_others")
            def act_step(n, attend, project, finish):
                v = [2 * n + (b + 1) for b in range(NB)]
                nxt = [2 * n + (b + 3) for b in range(NB)]
                prv = [2 * n + (b - 1) for b in range(NB)]

                def turn_x(b):
                    e.wait_ge(S["xnT_ps"], nxt[b])
                    e.activation(xnT[:, b, :], pa[b][:, 0:256], ACT.Copy).then_inc(S["xnT_d"], 1)

                def take_qk(b):
                    e.wait_ge(S["qkg_ps"], nxt[b])
                    e.activation(g1T[0:R, b, :], pa[b][0:R, 0:P], ACT.Copy).then_inc(S["g1T_d"], 1)
                    e.activation(qkT[:, b, :], pa[b][:, 256:512], ACT.Copy).then_inc(S["qkT_d"], 1)

                def softplus(b):
                    e.wait_ge(S["zg_ps"], nxt[b])
                    e.activation(zl[:, b, :], pa[b][:, 0:HALF + D], ACT.Abs).then_inc(S["za_d"], 1)
                    e.activation(zr[:, b, :], pa[b][:, 0:HALF + D], ACT.Relu, scale=-1.0).then_inc(S["zr_d"], 1)
                    e.wait_ge(S["za_d"], nxt[b])
                    e.activation(zl[:, b, :], zl[:, b, :], ACT.Exp, scale=-1.0).then_inc(S["ze_d"], 1)
                    e.activation(gs[:, b, :], pa[b][:, HALF:HALF + D], ACT.Copy).then_inc(S["gs_d"], 1)
                    e.wait_ge(S["ze_d"], nxt[b])
                    e.activation(zl[:, b, :], zl[:, b, :], ACT.Ln, bias=1.0).then_inc(S["zl_d"], 1)

                def decays(b):
                    if attend:
                        e.wait_ge(S["st_d"], v[b])
                    e.wait_ge(S["cum_ps"], nxt[b])
                    e.activation(e1[:, b, :], pc[b][:, 0:P], ACT.Exp, scale=-GK).then_inc(S["e1_d"], 1)
                    e.activation(e2[:, b, :], pc[b][:, 0:P], ACT.Exp, scale=GK).then_inc(S["e2_d"], 1)
                    e.activation(e3[:, b, :], pc[b][:, P:P + HALF], ACT.Exp, scale=-GK).then_inc(S["e3_d"], 1)
                    e.activation(sgm[:, b, :], zr[:, b, HALF:HALF + D], ACT.Exp, scale=-1.0).then_inc(S["sgm_d"], 1)

                def turn_o(b):
                    e.wait_ge(S["ogT_ps"], v[b])
                    e.activation(ogT[:, b, :], py[b][:, 0:256], ACT.Copy).then_inc(S["ogT_d"], 1)

                def squares(b):
                    e.wait_ge(S["mean2_d"], v[b])
                    e.activation(sq2[:, b, :], x2[:, b, :], ACT.Square, bias=negmean2[:, b, :], accum_out=ssq2[:, b, :]).then_inc(S["ssq2_d"], 1)

                def head_scale(b):
                    e.wait_ge(S["hvar_d"], v[b])
                    e.activation(hvar[:, b, :], hvar[:, b, :], ACT.Ln, scale=1.0 / DV, bias=eps_col[:]).then_inc(S["hvs_d"], 1)
                    e.wait_ge(S["hvs_d"], v[b])
                    e.activation(hrs[:, b, :], hvar[:, b, :], ACT.Exp, scale=-0.5).then_inc(S["hrs_d"], 1)

                def row_scale(b):
                    e.wait_ge(S["ssq2_d"], v[b])
                    e.activation(vare2[:, b, :], ssq2[:, b, :], ACT.Ln, scale=1.0 / D, bias=eps_col[:]).then_inc(S["vare2_d"], 1)
                    e.wait_ge(S["vare2_d"], v[b])
                    e.activation(rstd2[:, b, :], vare2[:, b, :], ACT.Exp, scale=-0.5).then_inc(S["rstd2_d"], 1)

                def turn_x2(b):
                    e.wait_ge(S["x2nT_ps"], prv[b])
                    e.activation(x2nT[:, b, :], py[b][:, 0:256], ACT.Copy).then_inc(S["x2nT_d"], 1)
                if project:
                    turn_x(0)
                    turn_x(1)
                    take_qk(0)
                if finish:
                    turn_x2(0)
                    turn_x2(1)
                if project:
                    take_qk(1)
                if attend:
                    head_scale(0)
                if project:
                    softplus(0)
                if attend:
                    head_scale(1)
                    turn_o(0)
                if project:
                    softplus(1)
                    decays(0)
                if attend:
                    squares(0)
                    row_scale(0)
                    turn_o(1)
                if project:
                    decays(1)
                if attend:
                    squares(1)
                    row_scale(1)
            e.wait_ge(S["const"], 9)
            act_step(-1, False, True, False)
            act_step(0, True, True, False)
            with e.Fori(1, NCH - 1) as n:
                act_step(n, True, True, True)
            act_step(NCH - 1, True, False, True)
            act_step(NCH, False, False, True)
            e.wait_ge(S["shift_d"], 1)
            e.activation(expo[:], shifted[:], ACT.Exp).then_inc(S["expo_d"], 1)
            e.preload_act_table_set("silu_and_others")
            e.wait_ge(S["x_ps"], 1)
            e.activation(xhi[:], pXT[:, 0:KD * P], ACT.Copy).then_inc(S["xhi_d"], 1)
            e.wait_ge(S["starts_d"], 2)

            def act_tile(i, first, split=None):
                if not first:
                    e.wait_ge(S["ht_ps"], i)
                    e.activation(hhi[:], pHT[:], ACT.Copy).then_inc(S["hhi_d"], 1)
                    e.wait_ge(S["hid_d"], i)
                e.wait_ge(S["g_ps"], i + 1)
                e.activation(gact[:], pG[:], ACT.Silu).then_inc(S["sg_done"], 1)
                e.wait_ge(S["x_ps"], i + 2)
                e.activation(xhi[:], pXT[:, 0:KD * P], ACT.Copy).then_inc(S["xhi_d"], 1)
                if split is not None:
                    split_hi(*split)
                if not first:
                    sum_out(i)

            def sum_out(i):
                e.wait_ge(S["scat"], 16 * (i + (LAG - 2)))
                e.wait_ge(S["yps"], i)
                e.sem_inc(S["pass_"], 1)
                e.activation(ybuf[:, bass.ds(((i + (LAG - 1)) & 1) * D, D)], pY[:, 0:D], ACT.Copy).then_inc(S["yev"], 1)

            def act_pair(pr, first, more):
                for q in range(2):
                    ei = 2 * pr + q
                    t0 = e.value_load(starts[0:1, bass.ds(ei, 1)], min_val=MINT, max_val=NT * E) if not (first and q == 0) else 0
                    t1 = e.value_load(starts[0:1, bass.ds(ei + 1, 1)], min_val=MINT, max_val=NT * E)
                    for m in range(SPLIT):
                        act_tile(t0 + m, first and q == 0 and m == 0, (ei + 1, 1 - q, m) if more or q == 0 else None)
                    with e.Fori(t0 + SPLIT, t1) as i:
                        act_tile(i, False)

            act_pair(0, True, True)
            with e.Fori(1, E // 2 - 1) as pr:
                act_pair(pr, False, True)
            act_pair(E // 2 - 1, False, False)
            n_tiles = e.value_load(starts[0:1, E:E + 1], min_val=MINT * E, max_val=NT * E)
            e.wait_ge(S["ht_ps"], n_tiles)
            e.activation(hhi[:], pHT[:], ACT.Copy).then_inc(S["hhi_d"], 1)
            sum_out(n_tiles)
            e.wait_ge(S["scat"], 16 * (n_tiles + LAG))
            e.sem_inc(S["yev"], 1)

        @block.vector
        def _(e):
            def split_lo(ei, q, m):
                e.wait_ge(S["whi_d"], 3 * ei + (m + 1))
                e.tensor_tensor(wlo[q][:, m * WN:(m + 1) * WN], raw[:, m * WN:(m + 1) * WN],
                                whi[q][:, m * WN:(m + 1) * WN].bitcast(F32), ALU.subtract).then_inc(S["wlo_d"], 1)
            e.wait_ge(S["x_in"], 64)
            for m in range(SPLIT):
                split_lo(0, 0, m)
            with e.Fori(0, NCH) as n:
                for b in range(NB):
                    e.bn_stats(stats[:, b, bass.ds(n * 6, 6)], xs[:, b, bass.ds(n * D, D)]).then_inc(S["stats_d"], 1)
            e.wait_ge(S["stats_d"], 2 * NCH)
            for b in range(NB):
                for n in range(NCH):
                    e.bn_aggr(mv[:, b, n, :], stats[:, b, n * 6:n * 6 + 6]).then_inc(S["mv_d"], 1)
            e.wait_ge(S["mv_d"], 2 * NCH)
            e.tensor_scalar(vare[:], mv[:, :, :, 1], EPS, None, ALU.add).then_inc(S["vare_d"], 1)
            e.wait_ge(S["rstd_d"], 1)
            e.wait_ge(S["const"], 9)
            def normalise_chunk(b, m):
                e.tensor_scalar(xn[:, b, :], xs[:, b, bass.ds(m * D, D)], mv[:, b, bass.ds(m, 1), 0], rstd[:, b, bass.ds(m, 1)],
                                ALU.subtract, ALU.mult).then_inc(S["xn_d"], 1)

            def vec_step(n, attend, project, finish, ahead=False):
                v = [2 * n + (b + 1) for b in range(NB)]
                nxt = [2 * n + (b + 3) for b in range(NB)]
                prv = [2 * n + (b - 1) for b in range(NB)]

                def normalise(b):
                    e.wait_ge(S["xnT_ps"], nxt[b])
                    normalise_chunk(b, n + 2)

                def take_vk(b):
                    if attend:
                        e.wait_ge(S["so_ps"], v[b])
                    e.wait_ge(S["vk_ps"], nxt[b])
                    e.tensor_copy(vk[:, b, :], pc[b][:, 0:D + HALF]).then_inc(S["vk_d"], 1)

                def softplus(b):
                    e.wait_ge(S["zr_d"], nxt[b])
                    e.wait_ge(S["zl_d"], nxt[b])
                    e.tensor_tensor(zr[:, b, :], zr[:, b, :], zl[:, b, :], ALU.add).then_inc(S["gneg_d"], 1)

                def gate(b):
                    e.wait_ge(S["sgm_d"], nxt[b])
                    e.wait_ge(S["gs_d"], nxt[b])
                    e.tensor_tensor(sg[:, b, :], gs[:, b, :], sgm[:, b, :], ALU.mult).then_inc(S["sg_d"], 1)

                def decay(b):
                    e.wait_ge(S["qkT_d"], nxt[b])
                    e.wait_ge(S["e1_d"], nxt[b])
                    e.tensor_tensor(qd[:, b, :], qkT[:, b, 0:P], e1[:, b, :], ALU.mult).then_inc(S["qd_d"], 1)
                    e.wait_ge(S["e2_d"], nxt[b])
                    e.scalar_tensor_tensor(kn[:, b, :], qkT[:, b, P:2 * P], SCALING, e2[:, b, :], ALU.mult, ALU.mult).then_inc(S["kn_d"], 1)
                    e.wait_ge(S["e3_d"], nxt[b])
                    e.wait_ge(S["vk_d"], nxt[b])
                    e.scalar_tensor_tensor(kd[:, b, :], vk[:, b, D:D + HALF], SCALING, e3[:, b, :], ALU.mult, ALU.mult).then_inc(S["kd_d"], 1)

                def mask(b):
                    e.wait_ge(S["a_ps"], v[b])
                    e.tensor_tensor(am[:, b, :].rearrange("p (h i) -> p h i", h=H),
                                    pA[:].rearrange("p (h i) -> p h i", h=H),
                                    upto[:].unsqueeze(1).broadcast_to([P, H, P]), ALU.mult).then_inc(S["am_d"], 1)

                def centre(b):
                    e.wait_ge(S["so_ps"], v[b])
                    e.tensor_reduce(hsum[:, b, :], py[b][:, 0:D].rearrange("p (h v) -> p h v", h=H), AX.X, ALU.add).then_inc(S["hsum_d"], 1)
                    e.tensor_tensor(su[:, b, :], py[b][:, D:2 * D], head_block[:], ALU.mult).then_inc(S["su_d"], 1)
                    e.wait_ge(S["hsum_d"], v[b])
                    e.tensor_scalar(hmean[:, b, :], hsum[:, b, :], 1.0 / DV, None, ALU.mult).then_inc(S["hmean_d"], 1)
                    e.wait_ge(S["su_d"], v[b])
                    e.scalar_tensor_tensor(st[:, b, :], st[:, b, :], e1[:, b, P - 1:P], su[:, b, :], ALU.mult, ALU.add).then_inc(S["st_d"], 1)
                    e.wait_ge(S["hmean_d"], v[b])
                    e.tensor_tensor(oc[:, b, :].rearrange("p (h v) -> p h v", h=H), py[b][:, 0:D].rearrange("p (h v) -> p h v", h=H),
                                    hmean[:, b, :].unsqueeze(2).broadcast_to([P, H, DV]), ALU.subtract).then_inc(S["oc_d"], 1)

                def variance(b):
                    e.wait_ge(S["osq_d"], v[b])
                    e.tensor_reduce(hvar[:, b, :], osq[:, b, :].rearrange("p (h v) -> p h v", h=H), AX.X, ALU.add).then_inc(S["hvar_d"], 1)

                def gated(b):
                    e.wait_ge(S["hrs_d"], v[b])
                    e.tensor_tensor(on[:, b, :].rearrange("p (h v) -> p h v", h=H), oc[:, b, :].rearrange("p (h v) -> p h v", h=H),
                                    hrs[:, b, :].unsqueeze(2).broadcast_to([P, H, DV]), ALU.mult).then_inc(S["on_d"], 1)
                    e.wait_ge(S["on_d"], v[b])
                    e.wait_ge(S["sg_d"], v[b])
                    e.tensor_tensor(og[:, b, :], on[:, b, :], sg[:, b, :], ALU.mult).then_inc(S["og_d"], 1)

                def residual(b):
                    e.wait_ge(S[f"x2_st{b}"], 16 * n + 16)
                    e.wait_ge(S["y_ps"], v[b])
                    e.scalar_tensor_tensor(x2[:, b, :], py[b][:, D:2 * D], 1.0, xs[:, b, bass.ds(n * D, D)], ALU.mult, ALU.add, accum_out=sum2[:, b, :]).then_inc(S["x2_d"], 1)
                    e.wait_ge(S["x2_d"], v[b])
                    e.tensor_scalar(negmean2[:, b, :], sum2[:, b, :], -1.0 / D, None, ALU.mult).then_inc(S["mean2_d"], 1)

                def normalise2(b):
                    e.wait_ge(S[f"xn_st{b}"], 16 * (n - 1) + 16)
                    e.wait_ge(S["rstd2_d"], prv[b])
                    e.tensor_scalar(x2n[:, b, :], x2[:, b, :], negmean2[:, b, :], rstd2[:, b, :], ALU.add, ALU.mult).then_inc(S["x2n_d"], 1)

                def take_logits(b):
                    e.wait_ge(S["lg_ps"], prv[b])
                    e.tensor_copy(logits[:, b, bass.ds((n - 1) * E, E)], py[b][:, D:D + E]).then_inc(S["lg_d"], 1)
                if finish:
                    normalise2(0)
                if attend:
                    mask(0)
                if finish:
                    normalise2(1)
                if attend:
                    mask(1)
                if finish:
                    take_logits(0)
                    take_logits(1)
                if project:
                    take_vk(0)
                if attend:
                    centre(0)
                    variance(0)
                if ahead:
                    normalise(0)
                    normalise(1)
                if attend:
                    gated(0)
                if project:
                    take_vk(1)
                if attend:
                    centre(1)
                    variance(1)
                if project:
                    softplus(0)
                if attend:
                    gated(1)
                if project:
                    softplus(1)
                if attend:
                    residual(0)
                if project:
                    decay(0)
                    gate(0)
                if attend:
                    residual(1)
                if project:
                    decay(1)
                    gate(1)
            e.sem_inc(S["am_d"], 1)
            normalise_chunk(0, 0)
            normalise_chunk(1, 0)
            vec_step(-1, False, True, False, ahead=True)
            vec_step(0, True, True, False, ahead=True)
            with e.Fori(1, NCH - 2) as n:
                vec_step(n, True, True, True, ahead=True)
            vec_step(NCH - 2, True, True, True)
            vec_step(NCH - 1, True, False, True)
            vec_step(NCH, False, False, True)
            lg4 = logits[:].rearrange("p b (n c) -> p (b n) c", c=E)
            wide = lambda ap: ap.unsqueeze(2).broadcast_to([P, NT, E])
            e.wait_ge(S["lg_d"], NT)
            e.tensor_reduce(lmax[:], lg4, AX.X, ALU.max).then_inc(S["lmax_d"], 1)
            e.wait_ge(S["lmax_d"], 1)
            e.tensor_tensor(shifted[:], lg4, wide(lmax[:]), ALU.subtract).then_inc(S["shift_d"], 1)
            e.wait_ge(S["expo_d"], 1)
            e.tensor_reduce(lsum[:], expo[:], AX.X, ALU.add).then_inc(S["lsum_d"], 1)
            e.wait_ge(S["lsum_d"], 1)
            e.reciprocal(lrec[:], lsum[:]).then_inc(S["lrec_d"], 1)
            e.wait_ge(S["lrec_d"], 1)
            e.tensor_tensor(probs[:], expo[:], wide(lrec[:]), ALU.mult).then_inc(S["probs_d"], 1)
            e.wait_ge(S["probs_d"], 1)
            e.wait_ge(S["moe_c"], 9)
            mine = probs[:].unsqueeze(3).broadcast_to([P, NT, E, E])
            other = probs[:].unsqueeze(2).broadcast_to([P, NT, E, E])
            e.tensor_tensor(pq[:], other, mine, ALU.is_equal).then_inc(S["rank_d"], 1)
            e.tensor_tensor(pg[:], other, mine, ALU.is_gt).then_inc(S["rank_d"], 1)
            e.wait_ge(S["rank_d"], 1)
            e.tensor_tensor(pq[:], pq[:], earlier[:].unsqueeze(1).broadcast_to([P, NT, E, E]), ALU.mult).then_inc(S["rank_d"], 1)
            e.wait_ge(S["rank_d"], 3)
            e.tensor_tensor(pg[:], pg[:], pq[:], ALU.add).then_inc(S["rank_d"], 1)
            e.wait_ge(S["rank_d"], 4)
            e.tensor_tensor(pg[:], pg[:], other, ALU.mult).then_inc(S["rank_d"], 1)
            e.wait_ge(S["rank_d"], 5)
            e.tensor_reduce(before[:], pg[:], AX.X, ALU.add).then_inc(S["before_d"], 1)
            e.wait_ge(S["before_d"], 1)
            e.tensor_scalar(keep[:].rearrange("p c t -> p t c"), before[:], TOP_P, None, ALU.is_le).then_inc(S["keep_d"], 1)
            e.scalar_tensor_tensor(wts[:], before[:], TOP_P, probs[:], ALU.is_le, ALU.mult).then_inc(S["wts_d"], 1)
            e.wait_ge(S["pos_ps"], 1)
            e.tensor_copy(tot[:], pTot.rearrange("p (c t) -> p c t", c=E)).then_inc(S["tot_d"], 1)
            e.wait_ge(S["tot_d"], 1)
            src, k, cnt = tot, 1, 0
            while k < NT:
                dst = scan[cnt % 2]
                e.tensor_tensor(dst[:, :, k:], src[:, :, k:], src[:, :, :NT - k], ALU.add).then_inc(S["scan_d"], 1)
                e.tensor_copy(dst[:, :, :k], src[:, :, :k]).then_inc(S["scan_d"], 1)
                cnt += 1
                e.wait_ge(S["scan_d"], 2 * cnt)
                src, k = dst, 2 * k
            other_scan = scan[cnt % 2]
            e.tensor_tensor(other_scan[:], src[:], tot[:], ALU.subtract).then_inc(S["slot_d"], 1)
            e.tensor_scalar(tiles_i[:], src[:, :, NT - 1], float(P - 1), None, ALU.add).then_inc(S["slot_d"], 1)
            e.wait_ge(S["slot_d"], 2)
            e.tensor_tensor(slot[:], pPos.rearrange("p (c t) -> p c t", c=E), other_scan[:], ALU.add).then_inc(S["slot_d"], 1)
            e.tensor_scalar(tiles_s[:], tiles_i[:], 7, None, ALU.arith_shift_right).then_inc(S["slot_d"], 1)
            e.wait_ge(S["slot_d"], 4)
            e.scalar_tensor_tensor(slot[:], keep[:], -float(4 * TOK), slot[:], ALU.mult, ALU.add).then_inc(S["slot_d"], 1)
            e.tensor_scalar(tiles_f[0][:], tiles_s[:], float(MINT), None, ALU.max).then_inc(S["slot_d"], 1)
            e.wait_ge(S["slot_d"], 6)
            e.tensor_scalar(slot_i[:], slot[:], float(4 * TOK), None, ALU.add).then_inc(S["sloti_d"], 1)
            src, k, cnt2 = tiles_f[0], 1, 0
            while k < E:
                dst = tiles_f[(cnt2 + 1) % 2]
                e.tensor_tensor(dst[:, k:], src[:, k:], src[:, :E - k], ALU.add).then_inc(S["scan_d"], 1)
                e.tensor_copy(dst[:, :k], src[:, :k]).then_inc(S["scan_d"], 1)
                cnt2 += 1
                e.wait_ge(S["scan_d"], 2 * (cnt + cnt2))
                src, k = dst, 2 * k
            e.memset(starts[:, 0:1], 0).then_inc(S["starts_d"], 1)
            e.tensor_copy(starts[:, 1:E + 1], src[:]).then_inc(S["starts_d"], 1)
            e.wait_ge(S["starts_d"], 2)
            e.wait_ge(S["sloti_d"], 1)
            e.tensor_scalar(sb_i[:], slot_i[:], P - 1, None, ALU.bitwise_and).then_inc(S["slotba_d"], 1)
            e.tensor_scalar(sa_i[:], slot_i[:], 7, None, ALU.arith_shift_right).then_inc(S["slotba_d"], 1)
            e.wait_ge(S["slotba_d"], 2)
            e.tensor_copy(slot_b[:], sb_i[:].rearrange("p c t -> p (c t)")).then_inc(S["slotf_d"], 1)
            e.tensor_copy(slot_a[:], sa_i[:].rearrange("p c t -> p (c t)")).then_inc(S["slotf_d"], 1)
            e.wait_ge(S["slotf_d"], 2)

            def mark_tiles(ei):
                e.tensor_tensor(hot_a[:], slot_a[:, bass.ds(ei * NT, NT)].unsqueeze(2).broadcast_to([P, NT, NT]),
                                iota_a[:].unsqueeze(1).broadcast_to([P, NT, NT]), ALU.is_equal).then_inc(S["hota_d"], 1)
                e.wait_ge(S["hota_d"], ei + 1)
                e.tensor_tensor(id_a[:], hot_a[:], tok_id[:].unsqueeze(2).broadcast_to([P, NT, NT]), ALU.mult).then_inc(S["ida_d"], 1)

            def mark_places(ei, half):
                t0, n = half * (NT // 2), NT // 2
                e.tensor_tensor(hot_b[:, t0 * P:(t0 + n) * P].rearrange("p (t s) -> p t s", t=n),
                                slot_b[:, bass.ds(ei * NT + t0, n)].unsqueeze(2).broadcast_to([P, n, P]),
                                iota_b[:].unsqueeze(1).broadcast_to([P, n, P]), ALU.is_equal).then_inc(S["hotb_d"], 1)

            def write_list(ei, t0):
                e.wait_ge(S["list_ps"], ei + 1)
                e.tensor_scalar(empty[:], pList, 0.0, dummy[:], ALU.is_equal, ALU.mult).then_inc(S["empty_d"], 1)
                e.wait_ge(S["empty_d"], ei + 1)
                e.sem_inc(S["pass_v"], 1)
                e.scalar_tensor_tensor(flat[:, bass.ds(t0 + LAG, NT)], pList, -1.0, empty[:], ALU.add, ALU.add).then_inc(S["lists_d"], 1)
            mark_tiles(0)
            mark_places(0, 0)
            mark_places(0, 1)
            write_list(0, 0)
            mark_tiles(1)
            mark_places(1, 0)
            mark_places(1, 1)
            start1 = e.value_load(starts[0:1, 1:2], min_val=MINT, max_val=NT * E)
            write_list(1, start1)

            def take(i, first=False):
                e.wait_ge(S["gath0"], 16 * (i // 2 + 1))
                if not first:
                    e.wait_ge(S["gath1"], 16 * ((i + 1) // 2))
                e.sem_inc(S["pass_v"], 1)
                e.tensor_copy(xcur[:], xg[:, bass.ds((i & 1) * ROW, ROW)]).then_inc(S["take_d"], 1)

            def vec_x(i):
                e.wait_ge(S["xhi_d"], i + 1)
                e.tensor_tensor(xlo[:], pXT[:, 0:KD * P], xhi[:].bitcast(F32), ALU.subtract).then_inc(S["xlo_d"], 1)
                e.wait_ge(S["take_d"], i + 3)
                e.tensor_copy(wcur[:], xcur[:, D:ROW]).then_inc(S["wcur_d"], 1)

            def vec_take(i):
                e.wait_ge(S["x_ps"], i)
                e.wait_ge(S["wcur_d"], i)
                take(i)

            def vec_ht(i):
                e.wait_ge(S["hhi_d"], i)
                e.tensor_tensor(hlo[:], pHT[:], hhi[:].bitcast(F32), ALU.subtract).then_inc(S["hlo_d"], 1)

            def vec_tile(ei, i, first, list_at=None):
                if not first:
                    vec_ht(i)
                e.wait_ge(S["wcur_d"], i + 1)
                e.wait_ge(S["sg_done"], i + 1)
                e.wait_ge(S["u_ps"], i + 1)
                e.scalar_tensor_tensor(hid[:], gact[:], wcur[:, bass.ds(ei, 1)], pU[:], ALU.mult, ALU.mult).then_inc(S["hid_d"], 1)
                e.wait_ge(S["hid_d"], i + 1)
                vec_x(i + 1)
                if list_at is not None:
                    write_list(ei + 1, list_at)
                vec_take(i + 2)

            def vec_pair(pr, first, more):
                for q in range(2):
                    ei = 2 * pr + q
                    t0 = e.value_load(starts[0:1, bass.ds(ei, 1)], min_val=MINT, max_val=NT * E) if not (first and q == 0) else 0
                    t1 = e.value_load(starts[0:1, bass.ds(ei + 1, 1)], min_val=MINT, max_val=NT * E)
                    for m in range(SPLIT):
                        vec_tile(ei, t0 + m, first and q == 0 and m == 0, t1 if m == 0 and (not first or q == 1) and (more or q == 0) else None)
                        if more:
                            if m == 0:
                                mark_tiles(ei + 2)
                            else:
                                mark_places(ei + 2, m - 1)
                        if more or q == 0:
                            split_lo(ei + 1, 1 - q, m)
                    with e.Fori(t0 + SPLIT, t1) as i:
                        vec_tile(ei, i, False)
            take(0, first=True)
            vec_x(0)
            vec_take(1)
            vec_pair(0, True, True)
            with e.Fori(1, E // 2 - 1) as pr:
                vec_pair(pr, False, True)
            vec_pair(E // 2 - 1, False, False)
            n_tiles = e.value_load(starts[0:1, E:E + 1], min_val=MINT * E, max_val=NT * E)
            vec_ht(n_tiles)
            e.wait_ge(S["take_d"], n_tiles + 4)
            take(n_tiles + 2)

        @block.tensor
        def _(e):
            def proj(dst, lhs, rhs, done=None):
                for k in range(KD):
                    last = e.matmul(dst, lhs(k), rhs(k), start=(k == 0), stop=(k == KD - 1))
                return last
            for s in ("w_q", "w_k", "w_kg1", "w_v", "w_g", "w_o", "w_r"):
                e.wait_ge(S[s], 16)
            e.wait_ge(S["w_kg2"], 48)
            e.wait_ge(S["const"], 9)
            def pe_step(n, attend, project, finish):
                v = [2 * n + (b + 1) for b in range(NB)]
                nxt = [2 * n + (b + 3) for b in range(NB)]
                prv = [2 * n + (b - 1) for b in range(NB)]

                def xT(b):
                    return lambda k: xnT[:, b, k * P:(k + 1) * P]

                def turn(b, done, src, dst, value, out_name):
                    e.wait_ge(S[done], value)
                    for k in range(KD):
                        last = e.transpose(dst[:, k * P:(k + 1) * P], src[:, b, k * P:(k + 1) * P], ident[:])
                    last.then_inc(S[out_name], 1)

                def project_qkv(b):
                    e.wait_ge(S["xnT_d"], nxt[b])
                    proj(pa[b][0:R, 0:P], lambda k: wkg1[:, k, :], xT(b))
                    proj(pa[b][:, 256:256 + P], lambda k: wq[:, k, :], xT(b))
                    proj(pa[b][:, 256 + P:512], lambda k: wk[:, k, :], xT(b)).then_inc(S["qkg_ps"], 1)
                    proj(pc[b][:, 0:D], xT(b), lambda k: wv[:, k, :])
                    proj(pc[b][:, D:D + HALF], xT(b), lambda k: wk[:, k, :]).then_inc(S["vk_ps"], 1)

                def project_gates(b):
                    e.wait_ge(S["g1T_d"], nxt[b])
                    e.wait_ge(S["qkT_d"], nxt[b])
                    e.matmul(pa[b][:, 0:HALF + D], g1T[:, b, :], wkg2[:], start=True, stop=False, skip_group_check=True)
                    e.matmul(pa[b][:, HALF:HALF + D], xT(b)(0), wg[:, 0, :], start=False, stop=False, skip_group_check=True)
                    e.matmul(pa[b][:, HALF:HALF + D], xT(b)(1), wg[:, 1, :], start=False, stop=True, skip_group_check=True).then_inc(S["zg_ps"], 1)

                def cumulate(b):
                    e.wait_ge(S["vk_d"], nxt[b])
                    e.wait_ge(S["gneg_d"], nxt[b])
                    e.matmul(pc[b][:, 0:P], zr[:, b, 0:HALF], upto[:], start=True, stop=True)
                    e.matmul(pc[b][:, P:P + HALF], after[:], zr[:, b, 0:HALF], start=True, stop=True).then_inc(S["cum_ps"], 1)

                def scores(b):
                    e.wait_ge(S["qm_d"], v[b])
                    e.wait_ge(S["kn_d"], v[b])
                    e.wait_ge(S["am_d"], v[b])
                    for j in range(2):
                        last = e.matmul(pA[:, j * 512:(j + 1) * 512], kn[:, b, :], qm[:, b, j * 512:(j + 1) * 512], start=True, stop=True)
                    last.then_inc(S["a_ps"], 1)

                def outputs(b):
                    e.wait_ge(S["kd_d"], v[b])
                    e.wait_ge(S["vk_d"], v[b])
                    if finish:
                        e.wait_ge(S["lg_d"], prv[b])
                    e.matmul(py[b][:, D:2 * D], kd[:, b, :], vk[:, b, 0:D], start=True, stop=True)
                    e.matmul(py[b][:, 0:D], qd[:, b, :], st[:, b, :], start=True, stop=False, skip_group_check=True)
                    e.wait_ge(S["am_d"], v[b] + 1)
                    for h in range(H):
                        last = e.matmul(py[b][:, h * DV:(h + 1) * DV], am[:, b, h * P:(h + 1) * P], vk[:, b, h * DV:(h + 1) * DV],
                                        start=False, stop=(h == H - 1), skip_group_check=True)
                    last.then_inc(S["so_ps"], 1)

                def project_out(b):
                    e.wait_ge(S["ogT_d"], v[b])
                    proj(py[b][:, D:2 * D], lambda k: ogT[:, b, k * P:(k + 1) * P], lambda k: wo[:, k, :]).then_inc(S["y_ps"], 1)

                def route(b):
                    e.wait_ge(S["x2nT_d"], prv[b])
                    proj(py[b][:, D:D + E], lambda k: x2nT[:, b, k * P:(k + 1) * P], lambda k: rw_sb[:, k, :]).then_inc(S["lg_ps"], 1)
                if attend:
                    scores(0)
                if project:
                    turn(0, "xn_d", xn, pa[0], nxt[0], "xnT_ps")
                    turn(1, "xn_d", xn, pa[1], nxt[1], "xnT_ps")
                    project_qkv(0)
                if finish:
                    turn(0, "x2n_d", x2n, py[0], prv[0], "x2nT_ps")
                    turn(1, "x2n_d", x2n, py[1], prv[1], "x2nT_ps")
                if attend:
                    scores(1)
                if finish:
                    route(0)
                    route(1)
                if attend:
                    outputs(0)
                if project:
                    project_qkv(1)
                if attend:
                    outputs(1)
                if project:
                    project_gates(0)
                    project_gates(1)
                if attend:
                    turn(0, "og_d", og, py[0], v[0], "ogT_ps")
                if project:
                    cumulate(0)
                if attend:
                    project_out(0)
                    turn(1, "og_d", og, py[1], v[1], "ogT_ps")
                if project:
                    cumulate(1)
                if attend:
                    project_out(1)
            pe_step(-1, False, True, False)
            pe_step(0, True, True, False)
            with e.Fori(1, NCH - 1) as n:
                pe_step(n, True, True, True)
            pe_step(NCH - 1, True, False, True)
            pe_step(NCH, False, False, True)
            e.wait_ge(S["moe_c"], 9)
            e.wait_ge(S["keep_d"], 1)
            kp = keep[:].rearrange("p c t -> p (c t)")
            e.matmul(pPos, tril[:], kp, start=True, stop=True)
            e.matmul(pTot, ones[:], kp, start=True, stop=True).then_inc(S["pos_ps"], 1)
            def build_list(ei):
                e.wait_ge(S["ida_d"], ei + 1)
                e.wait_ge(S["hotb_d"], 2 * ei + 2)
                for t in range(NT):
                    last = e.matmul(pList, hot_b[:, t * P:(t + 1) * P], id_a[:, t, :], start=(t == 0), stop=(t == NT - 1))
                last.then_inc(S["list_ps"], 1)
            build_list(0)
            e.wait_ge(S["lists_d"], 1)
            build_list(1)

            def products(dst, parts, n, done):
                last = None
                for m, (a, w) in enumerate(parts):
                    last = e.matmul(dst, a, w, start=(m == 0), stop=(m == len(parts) - 1))
                last.then_inc(S[done], 1)

            def x_parts(q, m):
                for k in range(KD):
                    c = slice(k * P, (k + 1) * P)
                    w = slice(m * WN + k * I, m * WN + (k + 1) * I)
                    yield xhi[:, c], whi[q][:, w]
                    yield xhi[:, c], wlo[q][:, w]
                    yield xlo[:, c], whi[q][:, w]

            def h_parts(q):
                for k in range(IC):
                    c = slice(k * P, (k + 1) * P)
                    w = slice(2 * WN + k * D, 2 * WN + (k + 1) * D)
                    yield hhi[:, c], whi[q][:, w]
                    yield hhi[:, c], wlo[q][:, w]
                    yield hlo[:, c], whi[q][:, w]

            def turn_x(i):
                e.wait_ge(S["take_d"], i + 3)
                for k in range(KD):
                    last = e.transpose(pXT[:, k * P:(k + 1) * P], xcur[:, k * P:(k + 1) * P], ident[:])
                last.then_inc(S["x_ps"], 1)

            def turn_h(i):
                e.wait_ge(S["hid_d"], i)
                for k in range(IC):
                    last = e.transpose(pHT[:, k * P:(k + 1) * P], hid[:, k * P:(k + 1) * P], ident[:])
                last.then_inc(S["ht_ps"], 1)

            def down(i, q):
                e.wait_ge(S["hlo_d"], i)
                e.wait_ge(S["yev"], i + 1)
                products(pY[:, 0:D], list(h_parts(q)), D, "yps")

            def pe_tile(i, q, q_before, first, next_list=None):
                if not first:
                    turn_h(i)
                e.wait_ge(S["xlo_d"], i + 1)
                if not first:
                    e.wait_ge(S["sg_done"], i)
                products(pG, list(x_parts(q, 0)), I, "g_ps")
                if next_list is not None:
                    build_list(next_list)
                products(pU, list(x_parts(q, 1)), I, "u_ps")
                turn_x(i + 1)
                if not first:
                    down(i, q_before)

            def pe_pair(pr, first, more):
                for q in range(2):
                    ei = 2 * pr + q
                    t0 = e.value_load(starts[0:1, bass.ds(ei, 1)], min_val=MINT, max_val=NT * E) if not (first and q == 0) else 0
                    t1 = e.value_load(starts[0:1, bass.ds(ei + 1, 1)], min_val=MINT, max_val=NT * E)
                    e.wait_ge(S["wlo_d"], 3 * ei + 3)
                    pe_tile(t0, q, 1 - q, first and q == 0, ei + 1 if (not first or q == 1) and (more or q == 0) else None)
                    for m in range(1, SPLIT):
                        pe_tile(t0 + m, q, q, False)
                    with e.Fori(t0 + SPLIT, t1) as i:
                        pe_tile(i, q, q, False)
            e.wait_ge(S["starts_d"], 2)
            turn_x(0)
            pe_pair(0, True, True)
            with e.Fori(1, E // 2 - 1) as pr:
                pe_pair(pr, False, True)
            pe_pair(E // 2 - 1, False, False)
            n_tiles = e.value_load(starts[0:1, E:E + 1], min_val=MINT * E, max_val=NT * E)
            turn_h(n_tiles)
            down(n_tiles, 1)


_INS = ['L0_attn_x', 'L0_attn_Wq', 'L0_attn_Wk', 'L0_attn_Wkg1', 'L0_attn_Wkg2', 'L0_attn_bkg2', 'L0_attn_Wv', 'L0_attn_Wg',
        'L0_attn_bg', 'L0_attn_Wo', 'L0_ffn_router_w', 'L0_ffn_gate_w', 'L0_ffn_up_w', 'L0_ffn_down_w']


def kernel(**inputs):
    import numpy as _np
    import concourse.bacc as _bacc
    from concourse import mybir as _mybir
    from concourse.bass_utils import run_bass_kernel_spmd as _run

    nc = _bacc.Bacc("TRN2", target_bir_lowering=False, num_devices=1)
    arrays, args = {}, []
    for name in _INS:
        a = inputs[name]
        if name.startswith("L0_ffn"):
            a = _np.swapaxes(a, -1, -2)
        a = _np.ascontiguousarray(a)
        arrays[f"in_{name}_dram"] = a
        args.append(nc.dram_tensor(f"in_{name}_dram", a.shape, _mybir.dt.from_np(a.dtype), kind="ExternalInput").ap())
    args.append(nc.dram_tensor("out_0_dram", (2, 1024, 256), _mybir.dt.float32, kind="ExternalOutput").ap())
    gla_moe_layer(nc, *args)
    r = _run(nc, [arrays], core_ids=[0])
    return r.results[0]["out_0_dram"]
```

```python
import concourse.bass as bass
from concourse import mybir
from contextlib import ExitStack


def gla_moe_layer(nc, x, Wq, Wk, Wkg1, Wkg2, bkg2, Wv, Wg, bg, Wo, rw, gate_w, up_w, down_w, out):
    F32 = mybir.dt.float32
    ALU = mybir.AluOpType
    ACT = mybir.ActivationFunctionType
    AX = mybir.AxisListType
    P = 128
    NB, T, D = 2, 1024, 256
    NCH = T // P
    H = 8
    DK, DV = 128 // H, D // H
    HALF = D // 2
    KD = D // P
    R = 16
    E = 8
    SCALING = float(DV) ** -0.5
    GK = 1.0 / 16.0
    EPS = 1e-5
    TOP_P = 0.9
    F32R = mybir.dt.float32r
    F16 = mybir.dt.float16
    I32 = mybir.dt.int32
    U32 = mybir.dt.uint32
    NT = NB * NCH
    TOK = NB * T
    I = 512
    IC = I // P
    WN = KD * I
    ROW = D + E
    SPLIT = 3
    MINT = SPLIT + 2
    LAG = 4

    rows = nc.dram_tensor("token_rows", (TOK + P, ROW), F32, kind="Internal").ap()
    sums = out.rearrange("b t d -> (b t) d")

    with ExitStack() as ctx:
        def sb(name, shape, dt=F32):
            return ctx.enter_context(nc.sbuf_tensor(name, shape, dt))

        def sem(name):
            return ctx.enter_context(nc.semaphore(name))

        xs = sb("xs", [P, NB, NCH * D])
        wq = sb("wq", [P, KD, HALF]); wk = sb("wk", [P, KD, HALF])
        wv = sb("wv", [P, KD, D]); wg = sb("wg", [P, KD, D]); wo = sb("wo", [P, KD, D])
        wkg1 = sb("wkg1", [P, KD, R]); wkg2 = sb("wkg2", [R + 1, HALF + D])
        rw_sb = sb("rw_sb", [P, KD, E])
        ident = sb("ident", [P, P]); upto = sb("upto", [P, P]); after = sb("after", [P, P])
        head_rows = sb("head_rows", [P, H]); head_block = sb("head_block", [P, D])
        stats = sb("stats", [P, NB, 6 * NCH]); mv = sb("mv", [P, NB, NCH, 2]); vare = sb("vare", [P, NB, NCH]); rstd = sb("rstd", [P, NB, NCH])
        x2 = sb("x2", [P, NB, D]); sum2 = sb("sum2", [P, NB, 1]); negmean2 = sb("negmean2", [P, NB, 1]); ssq2 = sb("ssq2", [P, NB, 1]); sq2 = sb("sq2", [P, NB, D]); vare2 = sb("vare2", [P, NB, 1]); rstd2 = sb("rstd2", [P, NB, 1])
        minus_half = sb("minus_half", [P, 2 * NCH]); eps_col = sb("eps_col", [P, 1])
        xn = sb("xn", [P, NB, D]); xnT = sb("xnT", [P, NB, KD * P])
        g1T = sb("g1T", [R + 1, NB, P]); qkT = sb("qkT", [P, NB, 2 * P])
        vk = sb("vk", [P, NB, D + HALF])
        work = sb("work", [P, NB * (2 * H * P + 9 * D)])
        taken = [0]

        def part(width):
            at = taken[0]
            taken[0] += NB * width
            return work[:, at:at + NB * width].rearrange("p (b n) -> p b n", b=NB)
        gs = part(D); sg = part(D); sgm = part(D); zl = part(HALF + D); zr = part(HALF + D)
        e1 = sb("e1", [P, NB, P]); e2 = sb("e2", [P, NB, P]); e3 = sb("e3", [P, NB, HALF])
        qd = sb("qd", [P, NB, P]); kn = sb("kn", [P, NB, P]); kd = sb("kd", [P, NB, HALF])
        qm = part(H * P); am = part(H * P)
        st = sb("st", [P, NB, D]); su = sb("su", [P, NB, D])
        hsum = sb("hsum", [P, NB, H]); hmean = sb("hmean", [P, NB, H])
        oc = part(D); osq = part(D); on = part(D)
        hvar = sb("hvar", [P, NB, H]); hrs = sb("hrs", [P, NB, H])
        og = sb("og", [P, NB, D]); ogT = sb("ogT", [P, NB, KD * P])
        x2n = sb("x2n", [P, NB, D]); x2nT = sb("x2nT", [P, NB, KD * P])
        logits = sb("logits", [P, NT, E])

        pe8 = lambda name, dt=F32: sb(name, [P, NT, E], dt)
        probs = pe8("probs"); expo = pe8("expo"); lmax = sb("lmax", [P, NT]); lsum = sb("lsum", [P, NT]); lrec = sb("lrec", [P, NT])
        shifted = pe8("shifted"); wts = pe8("wts"); before = sb("before", [P, NT, E]); 
        pg = sb("pg", [P, NT, E, E]); pq = sb("pq", [P, NT, E, E]); earlier = sb("earlier", [P, E, E])
        keep = sb("keep", [P, E, NT + 1], F16)
        slot = sb("slot", [P, E, NT]); slot_i = sb("slot_i", [P, E, NT], I32); sb_i = sb("sb_i", [P, E, NT], I32); sa_i = sb("sa_i", [P, E, NT], I32)
        slot_b = sb("slot_b", [P, E * NT], F16); slot_a = sb("slot_a", [P, E * NT])
        tril = sb("tril", [P, P], F16); ones = sb("ones", [P, P], F16)
        iota_b = sb("iota_b", [P, P], F16); iota_a = sb("iota_a", [P, NT]); tok_id = sb("tok_id", [P, NT]); dummy = sb("dummy_row", [P, 1])
        hot_a = sb("hot_a", [P, NT, NT]); id_a = sb("id_a", [P, NT, NT], F16); hot_b = work[:, 0:NT * P // 2].bitcast(F16)
        empty = sb("empty", [P, NT])
        tiles_i = sb("tiles_i", [P, E], I32); tiles_s = sb("tiles_s", [P, E], I32); tiles_f = [sb(f"tiles_f{i}", [P, E]) for i in range(2)]
        starts = sb("starts", [P, E + 1], I32)
        zrow = sb("zrow", [P, ROW])
        raw = sb("raw", [P, 3 * WN])
        whi = [sb(f"whi{q}", [P, 3 * WN], F32R) for q in range(2)]; wlo = [sb(f"wlo{q}", [P, 3 * WN], F32R) for q in range(2)]
        flat = sb("flat", [P, E * NT + NT + 2 * LAG], U32); idx_g = [sb(f"idx_g{u}", [P, 1], U32) for u in range(2)]; idx_s = [sb(f"idx_s{u}", [P, 1], U32) for u in range(2)]
        xg = sb("xg", [P, 2 * ROW]); xcur = sb("xcur", [P, ROW]); wcur = sb("wcur", [P, E])
        xhi = sb("xhi", [P, KD * P], F32R); xlo = sb("xlo", [P, KD * P], F32R)
        gact = sb("gact", [P, I]); hid = sb("hid", [P, I]); hhi = sb("hhi", [P, I], F32R); hlo = sb("hlo", [P, I], F32R)
        ybuf = sb("ybuf", [P, 2 * D])

        pa = [ctx.enter_context(nc.psum_tensor(f"pa{b}", [P, 512], F32)) for b in range(NB)]
        pc = [ctx.enter_context(nc.psum_tensor(f"pc{b}", [P, 512], F32)) for b in range(NB)]
        py = [ctx.enter_context(nc.psum_tensor(f"py{b}", [P, 512], F32)) for b in range(NB)]
        pA = ctx.enter_context(nc.psum_tensor("pA", [P, 1024], F32))

        S = {}
        for name in ("x_in x_rest w_q w_k w_kg1 w_kg2 wkg2_z eps_c w_v w_g w_o w_r const memz "
                     "stats_d mv_d vare_d vare2_d rstd_d xn_d xnT_ps xnT_d qkg_ps g1T_d qkT_d vk_ps vk_d "
                     "zg_ps za_d zr_d ze_d zl_d gneg_d ga_d gr_d ge_d gl_d gsum_d gs_d sgm_d sg_d cum_ps e1_d e2_d e3_d "
                     "qd_d kn_d kd_d qm_d a_ps am_d so_ps su_d st_d hsum_d hmean_d oc_d osq_d hvar_d hvs_d hrs_d "
                     "on_d og_d ogT_ps ogT_d y_ps x2_d x2_st0 x2_st1 mean2_d ssq2_d rstd2_d x2n_d x2nT_ps x2nT_d lg_ps lg_d "
                     "lmax_d shift_d expo_d lsum_d lrec_d probs_d rank_d before_d wts_d keep_d w_st rows_z pos_ps tot_d scan_d slot_d "
                     "sloti_d slotba_d slotf_d hota_d ida_d hotb_d list_ps empty_d lists_d starts_d xn_st0 xn_st1 "
                     "raw_in whi_d wlo_d gath0 gath1 flat_d idxg_d idxs_d x_ps xhi_d xlo_d wcur_d take_d g_ps sg_done u_ps hid_d ht_ps hhi_d hlo_d yps yev scat moe_c moe_z pass_ pass_v all_done").split():
            S[name] = sem(name)
        block = ctx.enter_context(nc.Block())

        pG = pA[:, 0:I]; pU = pA[:, I:2 * I]; pXT = pa[0]; pHT = pa[1]; pY = pc[0]
        pSlot = pc[0][:, 0:E * (NT + 1)].rearrange("p (c t) -> p c t", c=E); pList = pc[1][:, 0:NT]

        route_parts = (slice(0, NT - NB), slice(NT - NB, NT))

        @block.sync
        def _(e):
            e.dma_start(xs[:, :, 0:D], x[:, 0:P].rearrange("b p d -> p b d")).then_inc(S["x_in"], 16)
            e.wait_ge(S["w_v"], 16)
            for b in range(NB):
                e.dma_start(xs[:, b, D:].rearrange("p (n d) -> p n d", d=D),
                            x[b, P:].rearrange("(n p) d -> p n d", p=P)).then_inc(S["x_rest"], 16)
            def load_expert(ei):
                for m, w in enumerate((gate_w, up_w, down_w)):
                    e.dma_start(raw[:, m * WN:(m + 1) * WN].rearrange("p (c n) -> p c n", c=w.shape[1] // P),
                                w[bass.ds(ei, 1)].rearrange("a (c p) n -> p (a c) n", p=P)).then_inc(S["raw_in"], 16)
            e.wait_ge(S["w_o"], 16)
            load_expert(0)
            e.wait_ge(S["moe_z"], 1)
            e.dma_start(rows[TOK:TOK + P, :], zrow[:]).then_inc(S["rows_z"], 16)
            for b in range(NB):
                e.sem_inc(S[f"x2_st{b}"], 16)
                e.sem_inc(S[f"xn_st{b}"], 16)
            with e.Fori(0, NCH) as n:
                for b in range(NB):
                    r0 = b * T + n * P
                    e.wait_ge(S["x2_d"], 2 * n + (b + 1))
                    e.dma_start(sums[bass.ds(r0, P), :], x2[:, b, :]).then_inc(S[f"x2_st{b}"], 16)
                for b in range(NB):
                    r0 = b * T + n * P
                    e.wait_ge(S["x2n_d"], 2 * n + (b + 1))
                    e.dma_start(rows[bass.ds(r0, P), 0:D], x2n[:, b, :]).then_inc(S[f"xn_st{b}"], 16)
            for part, c in enumerate(route_parts):
                e.wait_ge(S["wts_d"], part + 1)
                for b in range(NB):
                    e.dma_start(rows[b * T:(b + 1) * T, D:ROW].rearrange("(n p) c -> p n c", p=P)[:, c.start // NB:c.stop // NB],
                                wts[:, c].rearrange("p (n b) c -> p n b c", b=NB)[:, :, b]).then_inc(S["w_st"], 16)
            with e.Fori(1, E) as ei:
                e.wait_ge(S["wlo_d"], 3 * ei)
                load_expert(ei)
            e.wait_ge(S["starts_d"], 2)
            n_tiles = e.value_load(starts[0:1, E:E + 1], min_val=MINT * E, max_val=NT * E)
            e.wait_ge(S["scat"], ((n_tiles + LAG + 1) // 2) * 32)
            e.sem_inc(S["all_done"], 1)

        @block.gpsimd
        def _(e):
            e.memset(eps_col[:], EPS).then_inc(S["eps_c"], 1)
            e.memset(g1T[:], 1.0).then_inc(S["const"], 1)
            e.memset(wkg2[:], 0.0).then_inc(S["wkg2_z"], 1)
            e.memset(minus_half[:], -0.5).then_inc(S["const"], 1)
            e.memset(ident[:], 0.0).then_inc(S["memz"], 1)
            e.memset(upto[:], 1.0).then_inc(S["memz"], 1)
            e.memset(after[:], 1.0).then_inc(S["memz"], 1)
            e.memset(head_rows[:], 1.0).then_inc(S["memz"], 1)
            e.memset(head_block[:], 1.0).then_inc(S["memz"], 1)
            e.memset(st[:], 0.0).then_inc(S["const"], 1)
            e.wait_ge(S["memz"], 5)
            e.affine_select(out=ident[:], in_=ident[:], compare_op=ALU.not_equal, fill=1.0, base=0,
                            pattern=[[-1, P]], channel_multiplier=1).then_inc(S["const"], 1)
            e.affine_select(out=upto[:], in_=upto[:], compare_op=ALU.is_ge, fill=0.0, base=0,
                            pattern=[[1, P]], channel_multiplier=-1).then_inc(S["const"], 1)
            e.affine_select(out=after[:], in_=after[:], compare_op=ALU.is_gt, fill=0.0, base=0,
                            pattern=[[-1, P]], channel_multiplier=1).then_inc(S["const"], 1)
            e.affine_select(out=head_rows[:], in_=head_rows[:], compare_op=ALU.is_ge, fill=0.0, base=0,
                            pattern=[[-DK, H]], channel_multiplier=1).then_inc(S["memz"], 1)
            e.affine_select(out=head_block[:], in_=head_block[:], compare_op=ALU.is_ge, fill=0.0, base=0,
                            pattern=[[-DK, H], [0, DV]], channel_multiplier=1).then_inc(S["memz"], 1)
            e.wait_ge(S["memz"], 7)
            e.affine_select(out=head_rows[:], in_=head_rows[:], compare_op=ALU.is_ge, fill=0.0, base=DK - 1,
                            pattern=[[DK, H]], channel_multiplier=-1).then_inc(S["const"], 1)
            e.affine_select(out=head_block[:], in_=head_block[:], compare_op=ALU.is_ge, fill=0.0, base=DK - 1,
                            pattern=[[DK, H], [0, DV]], channel_multiplier=-1).then_inc(S["const"], 1)
            def pool_step(n, attend, project, finish):
                v = [2 * n + (b + 1) for b in range(NB)]
                nxt = [2 * n + (b + 3) for b in range(NB)]
                prv = [2 * n + (b - 1) for b in range(NB)]
                if attend:
                    for b in range(NB):
                        e.wait_ge(S["oc_d"], v[b])
                        e.tensor_tensor(osq[:, b, :], oc[:, b, :], oc[:, b, :], ALU.mult).then_inc(S["osq_d"], 1)
                def spread_q(b):
                    e.wait_ge(S["qd_d"], nxt[b])
                    if attend:
                        e.wait_ge(S["a_ps"], v[b])
                    e.tensor_tensor(qm[:, b, :].rearrange("p (h i) -> p h i", h=H),
                                    qd[:, b, :].unsqueeze(1).broadcast_to([P, H, P]),
                                    head_rows[:].unsqueeze(2).broadcast_to([P, H, P]), ALU.mult).then_inc(S["qm_d"], 1)

                if project:
                    spread_q(0)
                    spread_q(1)
            e.wait_ge(S["const"], 8)
            pool_step(-1, False, True, False)
            e.memset(zrow[:], 0.0).then_inc(S["moe_z"], 1)
            e.memset(ybuf[:], 0.0).then_inc(S["moe_c"], 1)
            e.memset(keep[:], 0.0).then_inc(S["moe_c"], 1)
            e.memset(ones[:], 1.0).then_inc(S["moe_c"], 1)
            e.memset(tril[:], 1.0).then_inc(S["memz"], 1)
            e.memset(earlier[:], 1.0).then_inc(S["memz"], 1)
            e.iota(iota_b[:], pattern=[[1, P]], base=0, channel_multiplier=0, allow_small_or_imprecise_dtypes=True).then_inc(S["moe_c"], 1)
            e.iota(iota_a[:], pattern=[[1, NT]], base=0, channel_multiplier=0, allow_small_or_imprecise_dtypes=True).then_inc(S["moe_c"], 1)
            e.iota(tok_id[:], pattern=[[P, NCH], [T, NB]], base=1, channel_multiplier=1, allow_small_or_imprecise_dtypes=True).then_inc(S["moe_c"], 1)
            e.iota(dummy[:], pattern=[[1, 1]], base=TOK + 1, channel_multiplier=1, allow_small_or_imprecise_dtypes=True).then_inc(S["moe_c"], 1)
            e.iota(flat[:].bitcast(I32), pattern=[[0, E * NT + NT + 2 * LAG]], base=TOK, channel_multiplier=1).then_inc(S["moe_c"], 1)
            e.wait_ge(S["memz"], 9)
            e.affine_select(out=tril[:], in_=tril[:], compare_op=ALU.is_gt, fill=0.0, base=0,
                            pattern=[[1, P]], channel_multiplier=-1).then_inc(S["moe_c"], 1)
            e.affine_select(out=earlier[:], in_=earlier[:], compare_op=ALU.is_gt, fill=0.0, base=0,
                            pattern=[[1, E], [-1, E]], channel_multiplier=0).then_inc(S["moe_c"], 1)
            pool_step(0, True, True, False)
            with e.Fori(1, NCH - 1) as n:
                pool_step(n, True, True, True)
            pool_step(NCH - 1, True, False, True)
            pool_step(NCH, False, False, True)

            e.wait_ge(S["moe_c"], 10)
            e.sem_inc(S["yev"], LAG)
            e.sem_inc(S["take_d"], 2)
            e.wait_ge(S["w_st"], 16 * NB * len(route_parts))
            e.wait_ge(S["rows_z"], 16)
            for b in range(NB):
                e.wait_ge(S[f"x2_st{b}"], 16 * NCH + 16)
                e.wait_ge(S[f"xn_st{b}"], 16 * NCH + 16)
            e.wait_ge(S["lists_d"], 1)

            def gather(i, u):
                e.wait_ge(S["take_d"], i + 1)
                e.sem_inc(S["pass_"], 1)
                e.tensor_copy(idx_g[u][:], flat[:, bass.ds(i + LAG, 1)]).then_inc(S["idxg_d"], 1)
                e.wait_ge(S["idxg_d"], i + 1)
                e.sem_inc(S["pass_"], 1)
                e.indirect_dma_start(out=xg[:, u * ROW:(u + 1) * ROW], out_offset=None, in_=rows[:, :],
                                     in_offset=bass.IndirectOffsetOnAxis(ap=idx_g[u][:], axis=0)).then_inc(S[f"gath{u}"], 16)

            def scatter(i, u, first=False):
                e.wait_ge(S["yev"], i + 1)
                if not first:
                    e.wait_ge(S["scat"], 16 * i)
                e.sem_inc(S["pass_"], 1)
                e.tensor_copy(idx_s[u][:], flat[:, bass.ds(i, 1)]).then_inc(S["idxs_d"], 1)
                e.wait_ge(S["idxs_d"], i + 1)
                e.sem_inc(S["pass_"], 1)
                e.indirect_dma_start(out=sums[:, :], out_offset=bass.IndirectOffsetOnAxis(ap=idx_s[u][:], axis=0),
                                     in_=ybuf[:, u * D:(u + 1) * D], in_offset=None, compute_op=ALU.add,
                                     bounds_check=TOK - 1, oob_is_err=False).then_inc(S["scat"], 16)

            gather(0, 0)
            gather(1, 1)
            scatter(0, 0, first=True)
            scatter(1, 1)
            e.wait_ge(S["starts_d"], 2)
            n_tiles = e.value_load(starts[0:1, E:E + 1], min_val=MINT * E, max_val=NT * E)
            with e.Fori(1, (n_tiles + LAG + 1) // 2) as j:
                for u in range(2):
                    gather(2 * j + u, u)
                    scatter(2 * j + u, u)

        @block.scalar
        def _(e):
            def load_weight(dst, src, s):
                e.dma_start(dst[:], src.rearrange("(k p) n -> p k n", p=P)).then_inc(S[s], 16)
            load_weight(wkg1, Wkg1, "w_kg1")
            load_weight(wq, Wq, "w_q")
            load_weight(wk, Wk, "w_k")
            load_weight(wv, Wv, "w_v")
            e.preload_act_table_set("natural_log_exp_and_others")
            e.wait_ge(S["wkg2_z"], 1)
            e.dma_start(wkg2[0:R, 0:HALF], Wkg2).then_inc(S["w_kg2"], 16)
            e.dma_start(wkg2[R:R + 1, 0:HALF], bkg2.rearrange("(a n) -> a n", a=1)).then_inc(S["w_kg2"], 16)
            e.dma_start(wkg2[R:R + 1, HALF:HALF + D], bg.rearrange("(a n) -> a n", a=1)).then_inc(S["w_kg2"], 16)
            load_weight(wg, Wg, "w_g")
            load_weight(wo, Wo, "w_o")
            load_weight(rw_sb, rw, "w_r")
            def split_hi(ei, q, m):
                e.wait_ge(S["raw_in"], 48 * ei + 48)
                e.activation(whi[q][:, m * WN:(m + 1) * WN], raw[:, m * WN:(m + 1) * WN], ACT.Copy).then_inc(S["whi_d"], 1)
            def input_scale(part, chunks):
                e.wait_ge(S["mv_d"], NB if part == 0 else NB * NCH)
                e.activation(vare[:, :, chunks], mv[:, :, chunks, 1], ACT.Ln, bias=eps_col[:]).then_inc(S["vare_d"], 1)
                e.wait_ge(S["vare_d"], part + 1)
                e.activation(rstd[:, :, chunks], vare[:, :, chunks], ACT.Exp, scale=-0.5).then_inc(S["rstd_d"], 1)
            e.wait_ge(S["eps_c"], 1)
            input_scale(0, slice(0, 1))
            def route_exp(part):
                c = route_parts[part]
                e.wait_ge(S["shift_d"], part + 1)
                e.activation(expo[:, c], shifted[:, c], ACT.Exp).then_inc(S["expo_d"], 1)

            def act_step(n, attend, project, finish):
                v = [2 * n + (b + 1) for b in range(NB)]
                nxt = [2 * n + (b + 3) for b in range(NB)]
                prv = [2 * n + (b - 1) for b in range(NB)]

                def turn_x(b):
                    e.wait_ge(S["xnT_ps"], nxt[b])
                    e.activation(xnT[:, b, :], pa[b][:, 0:256], ACT.Copy).then_inc(S["xnT_d"], 1)

                def take_qk(b):
                    e.wait_ge(S["qkg_ps"], nxt[b])
                    e.activation(g1T[0:R, b, :], pa[b][0:R, 0:P], ACT.Copy).then_inc(S["g1T_d"], 1)
                    e.activation(qkT[:, b, :], pa[b][:, 256:512], ACT.Copy).then_inc(S["qkT_d"], 1)

                def softplus(b):
                    e.wait_ge(S["zg_ps"], nxt[b])
                    e.activation(zl[:, b, 0:HALF], pa[b][:, 0:HALF], ACT.Abs).then_inc(S["za_d"], 1)
                    e.activation(zr[:, b, 0:HALF], pa[b][:, 0:HALF], ACT.Relu, scale=-1.0).then_inc(S["zr_d"], 1)
                    e.wait_ge(S["za_d"], nxt[b])
                    e.activation(zl[:, b, 0:HALF], zl[:, b, 0:HALF], ACT.Exp, scale=-1.0).then_inc(S["ze_d"], 1)
                    e.activation(zl[:, b, HALF:], pa[b][:, HALF:HALF + D], ACT.Abs).then_inc(S["ga_d"], 1)
                    e.wait_ge(S["ze_d"], nxt[b])
                    e.activation(zl[:, b, 0:HALF], zl[:, b, 0:HALF], ACT.Ln, bias=1.0).then_inc(S["zl_d"], 1)

                def take_gate(b):
                    e.activation(zr[:, b, HALF:], pa[b][:, HALF:HALF + D], ACT.Relu, scale=-1.0).then_inc(S["gr_d"], 1)
                    if attend:
                        e.wait_ge(S["sg_d"], v[b])
                    e.activation(gs[:, b, :], pa[b][:, HALF:HALF + D], ACT.Copy).then_inc(S["gs_d"], 1)

                def decays(b):
                    if attend:
                        e.wait_ge(S["st_d"], v[b])
                    e.wait_ge(S["cum_ps"], nxt[b])
                    e.activation(e1[:, b, :], pc[b][:, 0:P], ACT.Exp, scale=-GK).then_inc(S["e1_d"], 1)
                    e.activation(e2[:, b, :], pc[b][:, 0:P], ACT.Exp, scale=GK).then_inc(S["e2_d"], 1)
                    e.activation(e3[:, b, :], pc[b][:, P:P + HALF], ACT.Exp, scale=-GK).then_inc(S["e3_d"], 1)

                def gate_softplus(b):
                    e.wait_ge(S["ga_d"], v[b])
                    e.activation(zl[:, b, HALF:], zl[:, b, HALF:], ACT.Exp, scale=-1.0).then_inc(S["ge_d"], 1)
                    e.wait_ge(S["ge_d"], v[b])
                    e.activation(zl[:, b, HALF:], zl[:, b, HALF:], ACT.Ln, bias=1.0).then_inc(S["gl_d"], 1)

                def gate_sigmoid(b):
                    e.wait_ge(S["gsum_d"], v[b])
                    e.activation(sgm[:, b, :], zr[:, b, HALF:], ACT.Exp, scale=-1.0).then_inc(S["sgm_d"], 1)

                def turn_o(b):
                    e.wait_ge(S["ogT_ps"], v[b])
                    e.activation(ogT[:, b, :], py[b][:, 0:256], ACT.Copy).then_inc(S["ogT_d"], 1)

                def squares(b):
                    e.wait_ge(S["mean2_d"], v[b])
                    e.activation(sq2[:, b, :], x2[:, b, :], ACT.Square, bias=negmean2[:, b, :], accum_out=ssq2[:, b, :]).then_inc(S["ssq2_d"], 1)

                def head_scale(b):
                    e.wait_ge(S["hvar_d"], v[b])
                    e.activation(hvar[:, b, :], hvar[:, b, :], ACT.Ln, scale=1.0 / DV, bias=eps_col[:]).then_inc(S["hvs_d"], 1)
                    e.wait_ge(S["hvs_d"], v[b])
                    e.activation(hrs[:, b, :], hvar[:, b, :], ACT.Exp, scale=-0.5).then_inc(S["hrs_d"], 1)

                def row_scale(b):
                    e.wait_ge(S["ssq2_d"], v[b])
                    e.activation(vare2[:, b, :], ssq2[:, b, :], ACT.Ln, scale=1.0 / D, bias=eps_col[:]).then_inc(S["vare2_d"], 1)
                    e.wait_ge(S["vare2_d"], v[b])
                    e.activation(rstd2[:, b, :], vare2[:, b, :], ACT.Exp, scale=-0.5).then_inc(S["rstd2_d"], 1)

                def turn_x2(b):
                    e.wait_ge(S["x2nT_ps"], prv[b])
                    e.activation(x2nT[:, b, :], py[b][:, 0:256], ACT.Copy).then_inc(S["x2nT_d"], 1)
                if project:
                    turn_x(0)
                    turn_x(1)
                if attend:
                    gate_softplus(0)
                    gate_softplus(1)
                if finish:
                    turn_x2(0)
                    turn_x2(1)
                if project:
                    take_qk(0)
                if attend:
                    gate_sigmoid(0)
                    gate_sigmoid(1)
                if finish and not project and attend:
                    route_exp(0)
                if project:
                    take_qk(1)
                if attend:
                    head_scale(0)
                if project:
                    softplus(0)
                    take_gate(0)
                if attend and project:
                    head_scale(1)
                    turn_o(0)
                if attend and not project:
                    turn_o(0)
                    head_scale(1)
                if project:
                    softplus(1)
                    decays(0)
                if attend:
                    turn_o(1)
                if project:
                    take_gate(1)
                if attend:
                    squares(0)
                    row_scale(0)
                if project:
                    decays(1)
                if attend:
                    squares(1)
                    row_scale(1)
            act_step(-1, False, True, False)
            input_scale(1, slice(1, NCH))
            split_hi(0, 0, 0)
            act_step(0, True, True, False)
            split_hi(0, 0, 1)
            with e.Fori(1, NCH - 1) as n:
                act_step(n, True, True, True)
            split_hi(0, 0, 2)
            act_step(NCH - 1, True, False, True)
            act_step(NCH, False, False, True)
            route_exp(1)
            e.preload_act_table_set("silu_and_others")
            e.wait_ge(S["x_ps"], 1)
            e.activation(xhi[:], pXT[:, 0:KD * P], ACT.Copy).then_inc(S["xhi_d"], 1)
            e.wait_ge(S["starts_d"], 2)

            def act_tile(i, first, split=None):
                if not first:
                    e.wait_ge(S["ht_ps"], i)
                    e.activation(hhi[:], pHT[:], ACT.Copy).then_inc(S["hhi_d"], 1)
                    e.wait_ge(S["hid_d"], i)
                e.wait_ge(S["g_ps"], i + 1)
                e.activation(gact[:], pG[:], ACT.Silu).then_inc(S["sg_done"], 1)
                e.wait_ge(S["x_ps"], i + 2)
                e.activation(xhi[:], pXT[:, 0:KD * P], ACT.Copy).then_inc(S["xhi_d"], 1)
                if split is not None:
                    split_hi(*split)
                if not first:
                    sum_out(i)

            def sum_out(i):
                e.wait_ge(S["scat"], 16 * (i + (LAG - 2)))
                e.wait_ge(S["yps"], i)
                e.sem_inc(S["pass_"], 1)
                e.activation(ybuf[:, bass.ds(((i + (LAG - 1)) & 1) * D, D)], pY[:, 0:D], ACT.Copy).then_inc(S["yev"], 1)

            def act_pair(pr, first, more):
                for q in range(2):
                    ei = 2 * pr + q
                    t0 = e.value_load(starts[0:1, bass.ds(ei, 1)], min_val=MINT, max_val=NT * E) if not (first and q == 0) else 0
                    t1 = e.value_load(starts[0:1, bass.ds(ei + 1, 1)], min_val=MINT, max_val=NT * E)
                    for m in range(SPLIT):
                        act_tile(t0 + m, first and q == 0 and m == 0, (ei + 1, 1 - q, m) if more or q == 0 else None)
                    with e.Fori(t0 + SPLIT, t1) as i:
                        act_tile(i, False)

            act_pair(0, True, True)
            with e.Fori(1, E // 2 - 1) as pr:
                act_pair(pr, False, True)
            act_pair(E // 2 - 1, False, False)
            n_tiles = e.value_load(starts[0:1, E:E + 1], min_val=MINT * E, max_val=NT * E)
            e.wait_ge(S["ht_ps"], n_tiles)
            e.activation(hhi[:], pHT[:], ACT.Copy).then_inc(S["hhi_d"], 1)
            sum_out(n_tiles)
            e.wait_ge(S["scat"], 16 * (n_tiles + LAG))
            e.sem_inc(S["yev"], 1)

        @block.vector
        def _(e):
            def split_lo(ei, q, m):
                e.wait_ge(S["whi_d"], 3 * ei + (m + 1))
                e.tensor_tensor(wlo[q][:, m * WN:(m + 1) * WN], raw[:, m * WN:(m + 1) * WN],
                                whi[q][:, m * WN:(m + 1) * WN].bitcast(F32), ALU.subtract).then_inc(S["wlo_d"], 1)
            e.wait_ge(S["x_in"], 16)
            for b in range(NB):
                e.bn_stats(stats[:, b, 0:6], xs[:, b, 0:D]).then_inc(S["stats_d"], 1)
            e.wait_ge(S["stats_d"], NB)
            for b in range(NB):
                e.bn_aggr(mv[:, b, 0, :], stats[:, b, 0:6]).then_inc(S["mv_d"], 1)
            e.wait_ge(S["rstd_d"], 1)
            def normalise_chunk(b, m):
                e.tensor_scalar(xn[:, b, :], xs[:, b, bass.ds(m * D, D)], mv[:, b, bass.ds(m, 1), 0], rstd[:, b, bass.ds(m, 1)],
                                ALU.subtract, ALU.mult).then_inc(S["xn_d"], 1)

            def route_softmax(part):
                c = route_parts[part]
                lg = logits[:, c]
                wide = lambda ap: ap.unsqueeze(2).broadcast_to([P, c.stop - c.start, E])
                e.wait_ge(S["lg_d"], c.stop)
                e.tensor_reduce(lmax[:, c], lg, AX.X, ALU.max).then_inc(S["lmax_d"], 1)
                e.wait_ge(S["lmax_d"], part + 1)
                e.tensor_tensor(shifted[:, c], lg, wide(lmax[:, c]), ALU.subtract).then_inc(S["shift_d"], 1)
                e.wait_ge(S["expo_d"], part + 1)
                e.tensor_reduce(lsum[:, c], expo[:, c], AX.X, ALU.add).then_inc(S["lsum_d"], 1)
                e.wait_ge(S["lsum_d"], part + 1)
                e.reciprocal(lrec[:, c], lsum[:, c]).then_inc(S["lrec_d"], 1)
                e.wait_ge(S["lrec_d"], part + 1)
                e.tensor_tensor(probs[:, c], expo[:, c], wide(lrec[:, c]), ALU.mult).then_inc(S["probs_d"], 1)

            def route_rank(part, step):
                c = route_parts[part]
                shape = [P, c.stop - c.start, E, E]
                mine = probs[:, c].unsqueeze(3).broadcast_to(shape)
                other = probs[:, c].unsqueeze(2).broadcast_to(shape)
                if step == 0:
                    e.wait_ge(S["probs_d"], part + 1)
                    e.tensor_tensor(pq[:, c], other, mine, ALU.is_equal).then_inc(S["rank_d"], 1)
                if step == 1:
                    e.tensor_tensor(pg[:, c], other, mine, ALU.is_gt).then_inc(S["rank_d"], 1)
                if step == 2:
                    e.wait_ge(S["rank_d"], 5 * part + 1)
                    e.tensor_tensor(pq[:, c], pq[:, c], earlier[:].unsqueeze(1).broadcast_to(shape), ALU.mult).then_inc(S["rank_d"], 1)
                if step == 3:
                    e.wait_ge(S["rank_d"], 5 * part + 3)
                    e.tensor_tensor(pg[:, c], pg[:, c], pq[:, c], ALU.add).then_inc(S["rank_d"], 1)
                if step == 4:
                    e.wait_ge(S["rank_d"], 5 * part + 4)
                    e.tensor_tensor(pg[:, c], pg[:, c], other, ALU.mult).then_inc(S["rank_d"], 1)

            def route_keep(part):
                c = route_parts[part]
                e.wait_ge(S["rank_d"], 5 * part + 5)
                e.tensor_reduce(before[:, c], pg[:, c], AX.X, ALU.add).then_inc(S["before_d"], 1)
                e.wait_ge(S["before_d"], part + 1)
                e.tensor_scalar(keep[:, :, c].rearrange("p c t -> p t c"), before[:, c], TOP_P, None, ALU.is_le).then_inc(S["keep_d"], 1)
                e.scalar_tensor_tensor(wts[:, c], before[:, c], TOP_P, probs[:, c], ALU.is_le, ALU.mult).then_inc(S["wts_d"], 1)

            def vec_step(n, attend, project, finish, ahead=False, route=False):
                v = [2 * n + (b + 1) for b in range(NB)]
                nxt = [2 * n + (b + 3) for b in range(NB)]
                prv = [2 * n + (b - 1) for b in range(NB)]

                def normalise(b):
                    e.wait_ge(S["xnT_ps"], nxt[b])
                    normalise_chunk(b, n + 2)

                def take_vk(b):
                    if attend:
                        e.wait_ge(S["so_ps"], v[b])
                    e.wait_ge(S["vk_ps"], nxt[b])
                    e.tensor_copy(vk[:, b, :], pc[b][:, 0:D + HALF]).then_inc(S["vk_d"], 1)

                def softplus(b):
                    e.wait_ge(S["zr_d"], nxt[b])
                    e.wait_ge(S["zl_d"], nxt[b])
                    e.tensor_tensor(zr[:, b, 0:HALF], zr[:, b, 0:HALF], zl[:, b, 0:HALF], ALU.add).then_inc(S["gneg_d"], 1)

                def gate_softplus(b):
                    e.wait_ge(S["gr_d"], v[b])
                    e.wait_ge(S["gl_d"], v[b])
                    e.tensor_tensor(zr[:, b, HALF:], zr[:, b, HALF:], zl[:, b, HALF:], ALU.add).then_inc(S["gsum_d"], 1)

                def gate(b):
                    e.wait_ge(S["sgm_d"], v[b])
                    e.wait_ge(S["gs_d"], v[b])
                    e.tensor_tensor(sg[:, b, :], gs[:, b, :], sgm[:, b, :], ALU.mult).then_inc(S["sg_d"], 1)

                def decay(b):
                    e.wait_ge(S["qkT_d"], nxt[b])
                    e.wait_ge(S["e1_d"], nxt[b])
                    e.tensor_tensor(qd[:, b, :], qkT[:, b, 0:P], e1[:, b, :], ALU.mult).then_inc(S["qd_d"], 1)
                    e.wait_ge(S["e2_d"], nxt[b])
                    e.scalar_tensor_tensor(kn[:, b, :], qkT[:, b, P:2 * P], SCALING, e2[:, b, :], ALU.mult, ALU.mult).then_inc(S["kn_d"], 1)
                    e.wait_ge(S["e3_d"], nxt[b])
                    e.wait_ge(S["vk_d"], nxt[b])
                    e.scalar_tensor_tensor(kd[:, b, :], vk[:, b, D:D + HALF], SCALING, e3[:, b, :], ALU.mult, ALU.mult).then_inc(S["kd_d"], 1)

                def mask(b):
                    e.wait_ge(S["a_ps"], v[b])
                    e.tensor_tensor(am[:, b, :].rearrange("p (h i) -> p h i", h=H),
                                    pA[:].rearrange("p (h i) -> p h i", h=H),
                                    upto[:].unsqueeze(1).broadcast_to([P, H, P]), ALU.mult).then_inc(S["am_d"], 1)

                def centre(b):
                    e.wait_ge(S["so_ps"], v[b])
                    e.tensor_reduce(hsum[:, b, :], py[b][:, 0:D].rearrange("p (h v) -> p h v", h=H), AX.X, ALU.add).then_inc(S["hsum_d"], 1)
                    e.tensor_tensor(su[:, b, :], py[b][:, D:2 * D], head_block[:], ALU.mult).then_inc(S["su_d"], 1)
                    e.wait_ge(S["hsum_d"], v[b])
                    e.tensor_scalar(hmean[:, b, :], hsum[:, b, :], 1.0 / DV, None, ALU.mult).then_inc(S["hmean_d"], 1)
                    e.wait_ge(S["su_d"], v[b])
                    e.scalar_tensor_tensor(st[:, b, :], st[:, b, :], e1[:, b, P - 1:P], su[:, b, :], ALU.mult, ALU.add).then_inc(S["st_d"], 1)
                    e.wait_ge(S["hmean_d"], v[b])
                    e.tensor_tensor(oc[:, b, :].rearrange("p (h v) -> p h v", h=H), py[b][:, 0:D].rearrange("p (h v) -> p h v", h=H),
                                    hmean[:, b, :].unsqueeze(2).broadcast_to([P, H, DV]), ALU.subtract).then_inc(S["oc_d"], 1)

                def variance(b):
                    e.wait_ge(S["osq_d"], v[b])
                    e.tensor_reduce(hvar[:, b, :], osq[:, b, :].rearrange("p (h v) -> p h v", h=H), AX.X, ALU.add).then_inc(S["hvar_d"], 1)

                def gated(b):
                    e.wait_ge(S["hrs_d"], v[b])
                    e.tensor_tensor(on[:, b, :].rearrange("p (h v) -> p h v", h=H), oc[:, b, :].rearrange("p (h v) -> p h v", h=H),
                                    hrs[:, b, :].unsqueeze(2).broadcast_to([P, H, DV]), ALU.mult).then_inc(S["on_d"], 1)
                    e.wait_ge(S["on_d"], v[b])
                    e.wait_ge(S["sg_d"], v[b])
                    e.tensor_tensor(og[:, b, :], on[:, b, :], sg[:, b, :], ALU.mult).then_inc(S["og_d"], 1)

                def residual(b):
                    e.wait_ge(S[f"x2_st{b}"], 16 * n + 16)
                    e.wait_ge(S["y_ps"], v[b])
                    e.scalar_tensor_tensor(x2[:, b, :], py[b][:, D:2 * D], 1.0, xs[:, b, bass.ds(n * D, D)], ALU.mult, ALU.add, accum_out=sum2[:, b, :]).then_inc(S["x2_d"], 1)
                    e.wait_ge(S["x2_d"], v[b])
                    e.tensor_scalar(negmean2[:, b, :], sum2[:, b, :], -1.0 / D, None, ALU.mult).then_inc(S["mean2_d"], 1)

                def normalise2(b):
                    e.wait_ge(S[f"xn_st{b}"], 16 * (n - 1) + 16)
                    e.wait_ge(S["rstd2_d"], prv[b])
                    e.tensor_scalar(x2n[:, b, :], x2[:, b, :], negmean2[:, b, :], rstd2[:, b, :], ALU.add, ALU.mult).then_inc(S["x2n_d"], 1)

                def take_logits(b):
                    e.wait_ge(S["lg_ps"], prv[b])
                    e.tensor_copy(logits[:, bass.ds(NB * (n - 1) + b, 1), :], py[b][:, D:D + E].unsqueeze(1)).then_inc(S["lg_d"], 1)
                if finish:
                    normalise2(0)
                if finish:
                    normalise2(1)
                if attend:
                    mask(0)
                    gate_softplus(0)
                    gate_softplus(1)
                if finish and not attend:
                    route_rank(0, 4)
                    route_keep(0)
                if finish:
                    take_logits(0)
                    take_logits(1)
                if attend:
                    mask(1)
                    gate(0)
                    gate(1)
                if project:
                    take_vk(0)
                if attend:
                    centre(0)
                if route:
                    route_softmax(0)
                if attend:
                    variance(0)
                if ahead:
                    normalise(0)
                    normalise(1)
                if attend:
                    gated(0)
                if project:
                    take_vk(1)
                if attend:
                    centre(1)
                    if route:
                        route_rank(0, 0)
                    variance(1)
                if project:
                    softplus(0)
                if attend:
                    gated(1)
                if route:
                    route_rank(0, 1)
                if project:
                    softplus(1)
                if attend:
                    residual(0)
                if project:
                    decay(0)
                if route:
                    route_rank(0, 2)
                if attend:
                    residual(1)
                if route:
                    route_rank(0, 3)
                if project:
                    decay(1)
            e.sem_inc(S["am_d"], 1)
            normalise_chunk(0, 0)
            normalise_chunk(1, 0)
            e.wait_ge(S["x_rest"], 16 * NB)
            with e.Fori(1, NCH) as n:
                for b in range(NB):
                    e.bn_stats(stats[:, b, bass.ds(n * 6, 6)], xs[:, b, bass.ds(n * D, D)]).then_inc(S["stats_d"], 1)
            e.wait_ge(S["stats_d"], NB * NCH)
            for b in range(NB):
                for n in range(1, NCH):
                    e.bn_aggr(mv[:, b, n, :], stats[:, b, n * 6:n * 6 + 6]).then_inc(S["mv_d"], 1)
            e.wait_ge(S["const"], 8)
            vec_step(-1, False, True, False)
            e.wait_ge(S["rstd_d"], 2)
            e.wait_ge(S["xnT_ps"], NB)
            normalise_chunk(0, 1)
            normalise_chunk(1, 1)
            split_lo(0, 0, 0)
            vec_step(0, True, True, False, ahead=True)
            split_lo(0, 0, 1)
            with e.Fori(1, NCH - 2) as n:
                vec_step(n, True, True, True, ahead=True)
            vec_step(NCH - 2, True, True, True)
            split_lo(0, 0, 2)
            e.wait_ge(S["moe_c"], 10)
            vec_step(NCH - 1, True, False, True, route=True)
            vec_step(NCH, False, False, True)
            route_softmax(1)
            for step in range(5):
                route_rank(1, step)
            route_keep(1)
            e.wait_ge(S["pos_ps"], 1)
            e.tensor_scalar(tiles_i[:], pSlot[:, :, NT], float(P - 1), None, ALU.add).then_inc(S["slot_d"], 1)
            e.scalar_tensor_tensor(slot[:], keep[:, :, 0:NT], -float(4 * TOK), pSlot[:, :, 0:NT], ALU.mult, ALU.add).then_inc(S["slot_d"], 1)
            e.wait_ge(S["slot_d"], 2)
            e.tensor_scalar(tiles_s[:], tiles_i[:], 7, None, ALU.arith_shift_right).then_inc(S["slot_d"], 1)
            e.tensor_scalar(slot_i[:], slot[:], float(4 * TOK), None, ALU.add).then_inc(S["sloti_d"], 1)
            e.wait_ge(S["sloti_d"], 1)
            e.tensor_scalar(sb_i[:], slot_i[:], P - 1, None, ALU.bitwise_and).then_inc(S["slotba_d"], 1)
            e.tensor_scalar(sa_i[:], slot_i[:], 7, None, ALU.arith_shift_right).then_inc(S["slotba_d"], 1)
            e.wait_ge(S["slotba_d"], 2)
            e.tensor_copy(slot_b[:], sb_i[:].rearrange("p c t -> p (c t)")).then_inc(S["slotf_d"], 1)
            e.tensor_copy(slot_a[:], sa_i[:].rearrange("p c t -> p (c t)")).then_inc(S["slotf_d"], 1)
            e.wait_ge(S["slotf_d"], 2)

            def mark_tiles(ei):
                e.tensor_tensor(hot_a[:], slot_a[:, bass.ds(ei * NT, NT)].unsqueeze(2).broadcast_to([P, NT, NT]),
                                iota_a[:].unsqueeze(1).broadcast_to([P, NT, NT]), ALU.is_equal).then_inc(S["hota_d"], 1)
                e.wait_ge(S["hota_d"], ei + 1)
                e.tensor_tensor(id_a[:], hot_a[:], tok_id[:].unsqueeze(2).broadcast_to([P, NT, NT]), ALU.mult).then_inc(S["ida_d"], 1)

            def mark_places(ei, half):
                t0, n = half * (NT // 2), NT // 2
                e.tensor_tensor(hot_b[:, t0 * P:(t0 + n) * P].rearrange("p (t s) -> p t s", t=n),
                                slot_b[:, bass.ds(ei * NT + t0, n)].unsqueeze(2).broadcast_to([P, n, P]),
                                iota_b[:].unsqueeze(1).broadcast_to([P, n, P]), ALU.is_equal).then_inc(S["hotb_d"], 1)

            def write_list(ei, t0):
                e.wait_ge(S["list_ps"], ei + 1)
                e.tensor_scalar(empty[:], pList, 0.0, dummy[:], ALU.is_equal, ALU.mult).then_inc(S["empty_d"], 1)
                e.wait_ge(S["empty_d"], ei + 1)
                e.sem_inc(S["pass_v"], 1)
                e.scalar_tensor_tensor(flat[:, bass.ds(t0 + LAG, NT)], pList, -1.0, empty[:], ALU.add, ALU.add).then_inc(S["lists_d"], 1)
            mark_tiles(0)
            mark_places(0, 0)
            mark_places(0, 1)
            write_list(0, 0)
            e.wait_ge(S["slot_d"], 3)
            e.tensor_scalar(tiles_f[0][:], tiles_s[:], float(MINT), None, ALU.max).then_inc(S["slot_d"], 1)
            e.wait_ge(S["slot_d"], 4)
            src, k, cnt2 = tiles_f[0], 1, 0
            while k < E:
                dst = tiles_f[(cnt2 + 1) % 2]
                e.tensor_tensor(dst[:, k:], src[:, k:], src[:, :E - k], ALU.add).then_inc(S["scan_d"], 1)
                e.tensor_copy(dst[:, :k], src[:, :k]).then_inc(S["scan_d"], 1)
                cnt2 += 1
                e.wait_ge(S["scan_d"], 2 * cnt2)
                src, k = dst, 2 * k
            e.memset(starts[:, 0:1], 0).then_inc(S["starts_d"], 1)
            e.tensor_copy(starts[:, 1:E + 1], src[:]).then_inc(S["starts_d"], 1)
            e.wait_ge(S["starts_d"], 2)
            mark_tiles(1)
            mark_places(1, 0)

            def take(i, first=False):
                e.wait_ge(S["gath0"], 16 * (i // 2 + 1))
                if not first:
                    e.wait_ge(S["gath1"], 16 * ((i + 1) // 2))
                e.sem_inc(S["pass_v"], 1)
                e.tensor_copy(xcur[:], xg[:, bass.ds((i & 1) * ROW, ROW)]).then_inc(S["take_d"], 1)

            def vec_x(i):
                e.wait_ge(S["xhi_d"], i + 1)
                e.tensor_tensor(xlo[:], pXT[:, 0:KD * P], xhi[:].bitcast(F32), ALU.subtract).then_inc(S["xlo_d"], 1)
                e.wait_ge(S["take_d"], i + 3)
                e.tensor_copy(wcur[:], xcur[:, D:ROW]).then_inc(S["wcur_d"], 1)

            def vec_take(i):
                e.wait_ge(S["x_ps"], i)
                e.wait_ge(S["wcur_d"], i)
                take(i)

            def vec_ht(i):
                e.wait_ge(S["hhi_d"], i)
                e.tensor_tensor(hlo[:], pHT[:], hhi[:].bitcast(F32), ALU.subtract).then_inc(S["hlo_d"], 1)

            def vec_tile(ei, i, first, list_at=None, split=None):
                if not first:
                    vec_ht(i)
                if split is not None:
                    split_lo(*split)
                e.wait_ge(S["wcur_d"], i + 1)
                e.wait_ge(S["sg_done"], i + 1)
                e.wait_ge(S["u_ps"], i + 1)
                e.scalar_tensor_tensor(hid[:], gact[:], wcur[:, bass.ds(ei, 1)], pU[:], ALU.mult, ALU.mult).then_inc(S["hid_d"], 1)
                e.wait_ge(S["hid_d"], i + 1)
                vec_x(i + 1)
                if list_at is not None:
                    write_list(ei + 1, list_at)
                vec_take(i + 2)

            def vec_pair(pr, first, more):
                for q in range(2):
                    ei = 2 * pr + q
                    t0 = e.value_load(starts[0:1, bass.ds(ei, 1)], min_val=MINT, max_val=NT * E) if not (first and q == 0) else 0
                    t1 = e.value_load(starts[0:1, bass.ds(ei + 1, 1)], min_val=MINT, max_val=NT * E)
                    for m in range(SPLIT + 1):
                        last = not (more or q == 0)
                        vec_tile(ei, t0 + m, first and q == 0 and m == 0, t1 if m == 0 and not last else None,
                                 (ei + 1, 1 - q, m - 1) if m > 0 and not last else None)
                        if more and m == 0:
                            mark_tiles(ei + 2)
                        if more and m > 1:
                            mark_places(ei + 2, m - 2)
                    with e.Fori(t0 + SPLIT + 1, t1) as i:
                        vec_tile(ei, i, False)
            take(0, first=True)
            vec_x(0)
            mark_places(1, 1)
            vec_take(1)
            vec_pair(0, True, True)
            with e.Fori(1, E // 2 - 1) as pr:
                vec_pair(pr, False, True)
            vec_pair(E // 2 - 1, False, False)
            n_tiles = e.value_load(starts[0:1, E:E + 1], min_val=MINT * E, max_val=NT * E)
            vec_ht(n_tiles)
            e.wait_ge(S["take_d"], n_tiles + 4)
            take(n_tiles + 2)

        @block.tensor
        def _(e):
            def proj(dst, lhs, rhs, done=None):
                for k in range(KD):
                    last = e.matmul(dst, lhs(k), rhs(k), start=(k == 0), stop=(k == KD - 1))
                return last
            def keep_clock(count):
                for m in range(count):
                    e.matmul(pA[:, 0:D], ident[:], head_block[:], start=True, stop=True)
            e.wait_ge(S["const"], 8)
            keep_clock(3)
            def pe_step(n, attend, project, finish):
                v = [2 * n + (b + 1) for b in range(NB)]
                nxt = [2 * n + (b + 3) for b in range(NB)]
                prv = [2 * n + (b - 1) for b in range(NB)]

                def xT(b):
                    return lambda k: xnT[:, b, k * P:(k + 1) * P]

                def turn(b, done, src, dst, value, out_name):
                    e.wait_ge(S[done], value)
                    for k in range(KD):
                        last = e.transpose(dst[:, k * P:(k + 1) * P], src[:, b, k * P:(k + 1) * P], ident[:])
                    last.then_inc(S[out_name], 1)

                def project_qkv(b):
                    if not attend:
                        for s in ("w_kg1", "w_q", "w_k", "w_v"):
                            e.wait_ge(S[s], 16)
                    e.wait_ge(S["xnT_d"], nxt[b])
                    proj(pa[b][0:R, 0:P], lambda k: wkg1[:, k, :], xT(b))
                    proj(pa[b][:, 256:256 + P], lambda k: wq[:, k, :], xT(b))
                    proj(pa[b][:, 256 + P:512], lambda k: wk[:, k, :], xT(b)).then_inc(S["qkg_ps"], 1)
                    proj(pc[b][:, 0:D], xT(b), lambda k: wv[:, k, :])
                    proj(pc[b][:, D:D + HALF], xT(b), lambda k: wk[:, k, :]).then_inc(S["vk_ps"], 1)

                def project_gates(b):
                    if not attend:
                        e.wait_ge(S["w_kg2"], 48)
                        e.wait_ge(S["w_g"], 16)
                    e.wait_ge(S["g1T_d"], nxt[b])
                    e.wait_ge(S["qkT_d"], nxt[b])
                    e.matmul(pa[b][:, 0:HALF + D], g1T[:, b, :], wkg2[:], start=True, stop=False, skip_group_check=True)
                    e.matmul(pa[b][:, HALF:HALF + D], xT(b)(0), wg[:, 0, :], start=False, stop=False, skip_group_check=True)
                    e.matmul(pa[b][:, HALF:HALF + D], xT(b)(1), wg[:, 1, :], start=False, stop=True, skip_group_check=True).then_inc(S["zg_ps"], 1)

                def cumulate(b):
                    e.wait_ge(S["vk_d"], nxt[b])
                    e.wait_ge(S["gneg_d"], nxt[b])
                    e.matmul(pc[b][:, 0:P], zr[:, b, 0:HALF], upto[:], start=True, stop=True)
                    e.matmul(pc[b][:, P:P + HALF], after[:], zr[:, b, 0:HALF], start=True, stop=True).then_inc(S["cum_ps"], 1)

                def scores(b):
                    e.wait_ge(S["qm_d"], v[b])
                    e.wait_ge(S["kn_d"], v[b])
                    e.wait_ge(S["am_d"], v[b])
                    for j in range(2):
                        last = e.matmul(pA[:, j * 512:(j + 1) * 512], kn[:, b, :], qm[:, b, j * 512:(j + 1) * 512], start=True, stop=True)
                    last.then_inc(S["a_ps"], 1)

                def outputs(b):
                    e.wait_ge(S["kd_d"], v[b])
                    e.wait_ge(S["vk_d"], v[b])
                    if finish:
                        e.wait_ge(S["lg_d"], prv[b])
                    e.matmul(py[b][:, D:2 * D], kd[:, b, :], vk[:, b, 0:D], start=True, stop=True)
                    e.matmul(py[b][:, 0:D], qd[:, b, :], st[:, b, :], start=True, stop=False, skip_group_check=True)
                    e.wait_ge(S["am_d"], v[b] + 1)
                    for h in range(H):
                        last = e.matmul(py[b][:, h * DV:(h + 1) * DV], am[:, b, h * P:(h + 1) * P], vk[:, b, h * DV:(h + 1) * DV],
                                        start=False, stop=(h == H - 1), skip_group_check=True)
                    last.then_inc(S["so_ps"], 1)

                def project_out(b):
                    e.wait_ge(S["ogT_d"], v[b])
                    proj(py[b][:, D:2 * D], lambda k: ogT[:, b, k * P:(k + 1) * P], lambda k: wo[:, k, :]).then_inc(S["y_ps"], 1)

                def route(b):
                    e.wait_ge(S["x2nT_d"], prv[b])
                    proj(py[b][:, D:D + E], lambda k: x2nT[:, b, k * P:(k + 1) * P], lambda k: rw_sb[:, k, :]).then_inc(S["lg_ps"], 1)
                if project:
                    if attend:
                        e.wait_ge(S["gs_d"], v[0])
                    turn(0, "xn_d", xn, pa[0], nxt[0], "xnT_ps")
                    if attend:
                        e.wait_ge(S["gs_d"], v[1])
                    turn(1, "xn_d", xn, pa[1], nxt[1], "xnT_ps")
                if attend:
                    scores(0)
                if finish:
                    turn(0, "x2n_d", x2n, py[0], prv[0], "x2nT_ps")
                    turn(1, "x2n_d", x2n, py[1], prv[1], "x2nT_ps")
                if project:
                    project_qkv(0)
                if finish:
                    route(0)
                    route(1)
                if attend:
                    scores(1)
                if attend:
                    outputs(0)
                if project:
                    project_qkv(1)
                if attend:
                    outputs(1)
                if project:
                    project_gates(0)
                    project_gates(1)
                if not attend and project:
                    keep_clock(6)
                if attend:
                    turn(0, "og_d", og, py[0], v[0], "ogT_ps")
                if project:
                    cumulate(0)
                if attend:
                    project_out(0)
                    turn(1, "og_d", og, py[1], v[1], "ogT_ps")
                if project:
                    cumulate(1)
                if attend:
                    project_out(1)
            pe_step(-1, False, True, False)
            keep_clock(5)
            e.wait_ge(S["w_o"], 16)
            e.wait_ge(S["w_r"], 16)
            pe_step(0, True, True, False)
            with e.Fori(1, NCH - 1) as n:
                pe_step(n, True, True, True)
            def count_kept(part):
                c = route_parts[part]
                e.wait_ge(S["moe_c"], 10)
                e.wait_ge(S["keep_d"], part + 1)
                if part == 0:
                    e.matmul(pSlot[:, :, c.stop:], tril[:], keep[:, :, NT:].broadcast_to([P, E, NT + 1 - c.stop]), start=True, stop=False, skip_group_check=True)
                e.matmul(pSlot[:, :, c], tril[:], keep[:, :, c], start=(part == 0), stop=False, skip_group_check=True)
                for t in range(c.start, c.stop):
                    last = e.matmul(pSlot[:, :, t + 1:], ones[:], keep[:, :, t:t + 1].broadcast_to([P, E, NT - t]),
                                    start=False, stop=(t == NT - 1), skip_group_check=True)
                if part == 1:
                    last.then_inc(S["pos_ps"], 1)
            pe_step(NCH - 1, True, False, True)
            pe_step(NCH, False, False, True)
            count_kept(0)
            count_kept(1)
            keep_clock(4)

            def build_list(ei):
                e.wait_ge(S["ida_d"], ei + 1)
                e.wait_ge(S["hotb_d"], 2 * ei + 2)
                for t in range(NT):
                    last = e.matmul(pList, hot_b[:, t * P:(t + 1) * P], id_a[:, t, :], start=(t == 0), stop=(t == NT - 1))
                last.then_inc(S["list_ps"], 1)
            build_list(0)
            keep_clock(9)

            def products(dst, parts, n, done):
                last = None
                for m, (a, w) in enumerate(parts):
                    last = e.matmul(dst, a, w, start=(m == 0), stop=(m == len(parts) - 1))
                last.then_inc(S[done], 1)

            def x_parts(q, m):
                for k in range(KD):
                    c = slice(k * P, (k + 1) * P)
                    w = slice(m * WN + k * I, m * WN + (k + 1) * I)
                    yield xhi[:, c], whi[q][:, w]
                    yield xhi[:, c], wlo[q][:, w]
                    yield xlo[:, c], whi[q][:, w]

            def h_parts(q):
                for k in range(IC):
                    c = slice(k * P, (k + 1) * P)
                    w = slice(2 * WN + k * D, 2 * WN + (k + 1) * D)
                    yield hhi[:, c], whi[q][:, w]
                    yield hhi[:, c], wlo[q][:, w]
                    yield hlo[:, c], whi[q][:, w]

            def turn_x(i):
                e.wait_ge(S["take_d"], i + 3)
                for k in range(KD):
                    last = e.transpose(pXT[:, k * P:(k + 1) * P], xcur[:, k * P:(k + 1) * P], ident[:])
                last.then_inc(S["x_ps"], 1)

            def turn_h(i):
                e.wait_ge(S["hid_d"], i)
                for k in range(IC):
                    last = e.transpose(pHT[:, k * P:(k + 1) * P], hid[:, k * P:(k + 1) * P], ident[:])
                last.then_inc(S["ht_ps"], 1)

            def down(i, q):
                e.wait_ge(S["hlo_d"], i)
                e.wait_ge(S["yev"], i + 1)
                products(pY[:, 0:D], list(h_parts(q)), D, "yps")

            def pe_tile(i, q, q_before, first, next_list=None):
                if not first:
                    turn_h(i)
                e.wait_ge(S["xlo_d"], i + 1)
                if not first:
                    e.wait_ge(S["sg_done"], i)
                products(pG, list(x_parts(q, 0)), I, "g_ps")
                if next_list is not None:
                    build_list(next_list)
                products(pU, list(x_parts(q, 1)), I, "u_ps")
                turn_x(i + 1)
                if not first:
                    down(i, q_before)

            def pe_pair(pr, first, more):
                for q in range(2):
                    ei = 2 * pr + q
                    t0 = e.value_load(starts[0:1, bass.ds(ei, 1)], min_val=MINT, max_val=NT * E) if not (first and q == 0) else 0
                    t1 = e.value_load(starts[0:1, bass.ds(ei + 1, 1)], min_val=MINT, max_val=NT * E)
                    e.wait_ge(S["wlo_d"], 3 * ei + 3)
                    pe_tile(t0, q, 1 - q, first and q == 0, ei + 1 if more or q == 0 else None)
                    for m in range(1, SPLIT):
                        pe_tile(t0 + m, q, q, False)
                    with e.Fori(t0 + SPLIT, t1) as i:
                        pe_tile(i, q, q, False)
            e.wait_ge(S["starts_d"], 2)
            turn_x(0)
            pe_pair(0, True, True)
            with e.Fori(1, E // 2 - 1) as pr:
                pe_pair(pr, False, True)
            pe_pair(E // 2 - 1, False, False)
            n_tiles = e.value_load(starts[0:1, E:E + 1], min_val=MINT * E, max_val=NT * E)
            turn_h(n_tiles)
            down(n_tiles, 1)


_INS = ['L0_attn_x', 'L0_attn_Wq', 'L0_attn_Wk', 'L0_attn_Wkg1', 'L0_attn_Wkg2', 'L0_attn_bkg2', 'L0_attn_Wv', 'L0_attn_Wg',
        'L0_attn_bg', 'L0_attn_Wo', 'L0_ffn_router_w', 'L0_ffn_gate_w', 'L0_ffn_up_w', 'L0_ffn_down_w']


def kernel(**inputs):
    import numpy as _np
    import concourse.bacc as _bacc
    from concourse import mybir as _mybir
    from concourse.bass_utils import run_bass_kernel_spmd as _run

    nc = _bacc.Bacc("TRN2", target_bir_lowering=False, num_devices=1)
    arrays, args = {}, []
    for name in _INS:
        a = inputs[name]
        if name.startswith("L0_ffn"):
            a = _np.swapaxes(a, -1, -2)
        a = _np.ascontiguousarray(a)
        arrays[f"in_{name}_dram"] = a
        args.append(nc.dram_tensor(f"in_{name}_dram", a.shape, _mybir.dt.from_np(a.dtype), kind="ExternalInput").ap())
    args.append(nc.dram_tensor("out_0_dram", (2, 1024, 256), _mybir.dt.float32, kind="ExternalOutput").ap())
    gla_moe_layer(nc, *args)
    r = _run(nc, [arrays], core_ids=[0])
    return r.results[0]["out_0_dram"]
```
